# Optimizing a Trainium2 kernel written in Bass

```python
import numpy as np
import jax
import jax.numpy as jnp

def _softmax(x, axis=-1):
    return jax.nn.softmax(x, axis=axis)

def _gelu(x):
    return jax.nn.gelu(x, approximate=True)

def _silu(x):
    return jax.nn.silu(x)

def _sigmoid(x):
    return jax.nn.sigmoid(x)

def _layernorm(x, axis=-1, eps=1e-05):
    m = jnp.mean(x, axis=axis, keepdims=True)
    v = jnp.var(x, axis=axis, keepdims=True)
    return (x - m) / jnp.sqrt(v + eps)

def _scatter_add(tgt, idx, src, axis=0):
    return tgt.at[idx].add(src)

def _segment_sum(src, seg, n):
    return jax.ops.segment_sum(src, seg, n)
kernel_name = 'mk_decoder_preln_d1_seqx_r8_863f4c'

def setup_inputs(seed: int=0):
    np.random.seed(seed)
    _w = jnp.asarray

    def _rec_inputs():
        import jax
        import jax.numpy as jnp
        _rk = jax.random.key(seed)
        x = 6.313e-05 + 0.9998 * jax.random.normal(jax.random.fold_in(_rk, 1), (64, 64, 128), jnp.float32)
        _lenS = 64 - jax.random.randint(jax.random.fold_in(_rk, 7), (64,), 0, max(1, 64 // 4) + 1, jnp.int32)
        _lenS2 = 64 - jax.random.randint(jax.random.fold_in(_rk, 8), (64,), 0, max(1, 64 // 4) + 1, jnp.int32)
        _ctx_1024P = jax.random.normal(jax.random.fold_in(_rk, 11), (64, 16, 128), jnp.float32)
        _ctx_1024c = jax.random.dirichlet(jax.random.fold_in(_rk, 511), 0.3 * jnp.ones((16,), jnp.float32), (64, 64))
        _ctx_1024t = jnp.einsum('bsk,bkd->bsd', _ctx_1024c, _ctx_1024P)
        _ctx_1024t = _ctx_1024t * jax.lax.rsqrt(jnp.mean(jnp.square(_ctx_1024t)) + 1e-12) * 0.953939
        ctx_1024 = -0.000214406 + 1.00034 * (_ctx_1024t + 0.3 * jax.random.normal(jax.random.fold_in(_rk, 611), (64, 64, 128), jnp.float32))
        return (x, ctx_1024)
    x, ctx_1024 = _rec_inputs()

    def _L0_attn_setup():
        import jax, jax.numpy as jnp
        import numpy as np
        D = 128
        B, T = (4, 256)

        def _scan_combine(c1, c2):
            a1, b1 = c1
            a2, b2 = c2
            return (a2 * a1, a2 * b1 + b2)
        key = jax.random.key(seed)
        ks = jax.random.split(key, 7)
        s = 0.02
        return {'x': jax.random.normal(ks[0], (B, T, D), dtype=jnp.float32), 'W_in': s * jax.random.normal(ks[1], (2 * D, D), dtype=jnp.float32), 'b_in': jnp.zeros((2 * D,), dtype=jnp.float32), 'W_s': s * jax.random.normal(ks[2], (D, D), dtype=jnp.float32), 'b_s': jnp.zeros((D,), dtype=jnp.float32), 'W_o': s * jax.random.normal(ks[3], (D, D), dtype=jnp.float32), 'b_o': jnp.zeros((D,), dtype=jnp.float32)}
    _L0_attn_all = _L0_attn_setup()
    _L0_attn_in = {k: v for k, v in _L0_attn_all.items() if k in ('W_in', 'b_in', 'W_s', 'b_s', 'W_o', 'b_o')}
    del _L0_attn_all

    def _L0_xattn_setup():
        import jax, jax.numpy as jnp
        import numpy as np
        from jax import lax
        BIG = jnp.float32(1e+30)

        def _pairwise_euclidean(a, b):
            aa = jnp.sum(a * a, axis=-1)[:, None]
            bb = jnp.sum(b * b, axis=-1)[None, :]
            ab = a @ b.T
            return jnp.sqrt(jnp.maximum(aa + bb - 2.0 * ab, 0.0))

        def _dtw_cost(D):
            row0 = jnp.cumsum(D[0])

            def row_step(prev_row, d_row):
                first = d_row[0] + prev_row[0]

                def col_step(left, inp):
                    d_ij, up, diag = inp
                    r = d_ij + jnp.minimum(jnp.minimum(up, left), diag)
                    return (r, r)
                _, rest = lax.scan(col_step, first, (d_row[1:], prev_row[1:], prev_row[:-1]))
                row = jnp.concatenate([first[None], rest])
                return (row, row)
            _, rows = lax.scan(row_step, row0, D[1:])
            return jnp.concatenate([row0[None], rows], axis=0)

        def _backtrack(R, T1, T2):
            L = T1 + T2 - 1

            def step(carry, _):
                i, j, done = carry
                valid = jnp.logical_not(done)
                cd = jnp.where((i > 0) & (j > 0), R[jnp.maximum(i - 1, 0), jnp.maximum(j - 1, 0)], BIG)
                cu = jnp.where(i > 0, R[jnp.maximum(i - 1, 0), j], BIG)
                cl = jnp.where(j > 0, R[i, jnp.maximum(j - 1, 0)], BIG)
                choice = jnp.argmin(jnp.stack([cd, cu, cl]))
                ni = jnp.where(choice <= 1, i - 1, i)
                nj = jnp.where((choice == 0) | (choice == 2), j - 1, j)
                at_origin = (i == 0) & (j == 0)
                ni = jnp.where(at_origin, 0, ni)
                nj = jnp.where(at_origin, 0, nj)
                return ((ni, nj, done | at_origin), (i, j, valid))
            init = (jnp.int32(T1 - 1), jnp.int32(T2 - 1), jnp.bool_(False))
            _, (i_idx, j_idx, valid) = lax.scan(step, init, None, length=L)
            return (i_idx, j_idx, valid)

        def _align_one(small, large):
            T_small, d = small.shape
            T_large = large.shape[0]
            D = _pairwise_euclidean(small, large)
            R = _dtw_cost(D)
            i_idx, j_idx, valid = _backtrack(R, T_small, T_large)
            contrib = small[i_idx] * valid[:, None].astype(small.dtype)
            expanded = jnp.zeros((T_large, d), dtype=small.dtype).at[j_idx].add(contrib)
            return expanded
        key = jax.random.key(seed)
        k1, k2 = jax.random.split(key)
        teacher = jax.random.normal(k1, (16, 50, 128), dtype=jnp.float32)
        student = jax.random.normal(k2, (16, 75, 128), dtype=jnp.float32)
        return {'teacher_features': teacher, 'student_features': student}
    _L0_xattn_all = _L0_xattn_setup()
    _L0_xattn_in = {k: v for k, v in _L0_xattn_all.items() if k in ()}
    del _L0_xattn_all

    def _L0_ffn_setup():
        import jax, jax.numpy as jnp
        import numpy as np
        B, T, C, I, E = (4, 256, 128, 352, 7)

        def _swiglu(h, w1, w2, w3):
            return jax.nn.silu(h @ w1.T) * (h @ w3.T) @ w2.T
        key = jax.random.key(seed)
        ks = jax.random.split(key, 9)
        sc_c = 1.0 / np.sqrt(C)
        sc_i = 1.0 / np.sqrt(I)
        return {'x': jax.random.normal(ks[0], (B, T, C), jnp.float32), 'router_w': jax.random.normal(ks[1], (E, C), jnp.float32) * sc_c, 'routing_bias': jnp.zeros((E,), jnp.float32), 'sw1': jax.random.normal(ks[2], (I, C), jnp.float32) * sc_c, 'sw2': jax.random.normal(ks[3], (C, I), jnp.float32) * sc_i, 'sw3': jax.random.normal(ks[4], (I, C), jnp.float32) * sc_c, 'ew1': jax.random.normal(ks[5], (E, I, C), jnp.float32) * sc_c, 'ew2': jax.random.normal(ks[6], (E, C, I), jnp.float32) * sc_i, 'ew3': jax.random.normal(ks[7], (E, I, C), jnp.float32) * sc_c}
    _L0_ffn_all = _L0_ffn_setup()
    _L0_ffn_in = {k: v for k, v in _L0_ffn_all.items() if k in ('router_w', 'routing_bias', 'sw1', 'sw2', 'sw3', 'ew1', 'ew2', 'ew3')}
    del _L0_ffn_all
    return {'x': x, 'ctx_1024': ctx_1024, 'L0_attn_W_in': _L0_attn_in['W_in'], 'L0_attn_b_in': _L0_attn_in['b_in'], 'L0_attn_W_s': _L0_attn_in['W_s'], 'L0_attn_b_s': _L0_attn_in['b_s'], 'L0_attn_W_o': _L0_attn_in['W_o'], 'L0_attn_b_o': _L0_attn_in['b_o'], 'L0_ffn_router_w': _L0_ffn_in['router_w'], 'L0_ffn_routing_bias': _L0_ffn_in['routing_bias'], 'L0_ffn_sw1': _L0_ffn_in['sw1'], 'L0_ffn_sw2': _L0_ffn_in['sw2'], 'L0_ffn_sw3': _L0_ffn_in['sw3'], 'L0_ffn_ew1': _L0_ffn_in['ew1'], 'L0_ffn_ew2': _L0_ffn_in['ew2'], 'L0_ffn_ew3': _L0_ffn_in['ew3']}

def reference(x, ctx_1024, L0_attn_W_in, L0_attn_b_in, L0_attn_W_s, L0_attn_b_s, L0_attn_W_o, L0_attn_b_o, L0_ffn_router_w, L0_ffn_routing_bias, L0_ffn_sw1, L0_ffn_sw2, L0_ffn_sw3, L0_ffn_ew1, L0_ffn_ew2, L0_ffn_ew3):
    import jax
    import jax.numpy as jnp

    def _L0_attn_ref(x, W_in, b_in, W_s, b_s, W_o, b_o):
        import jax, jax.numpy as jnp
        import numpy as np
        D = 128
        B, T = (4, 256)

        def _scan_combine(c1, c2):
            a1, b1 = c1
            a2, b2 = c2
            return (a2 * a1, a2 * b1 + b2)
        gv = jnp.einsum('btd,ed->bte', x, W_in) + b_in
        gate = jax.nn.sigmoid(gv[..., :D])
        val = gv[..., D:]
        sv = jnp.tanh(jnp.einsum('btd,ed->bte', val, W_s) + b_s)
        a = 1.0 - gate
        b = gate * sv
        _, h = jax.lax.associative_scan(_scan_combine, (a, b), axis=1)
        out = jnp.einsum('btd,ed->bte', h, W_o) + b_o
        return x + out

    def _L0_xattn_ref(teacher_features, student_features):
        import jax, jax.numpy as jnp
        import numpy as np
        from jax import lax
        BIG = jnp.float32(1e+30)

        def _pairwise_euclidean(a, b):
            aa = jnp.sum(a * a, axis=-1)[:, None]
            bb = jnp.sum(b * b, axis=-1)[None, :]
            ab = a @ b.T
            return jnp.sqrt(jnp.maximum(aa + bb - 2.0 * ab, 0.0))

        def _dtw_cost(D):
            row0 = jnp.cumsum(D[0])

            def row_step(prev_row, d_row):
                first = d_row[0] + prev_row[0]

                def col_step(left, inp):
                    d_ij, up, diag = inp
                    r = d_ij + jnp.minimum(jnp.minimum(up, left), diag)
                    return (r, r)
                _, rest = lax.scan(col_step, first, (d_row[1:], prev_row[1:], prev_row[:-1]))
                row = jnp.concatenate([first[None], rest])
                return (row, row)
            _, rows = lax.scan(row_step, row0, D[1:])
            return jnp.concatenate([row0[None], rows], axis=0)

        def _backtrack(R, T1, T2):
            L = T1 + T2 - 1

            def step(carry, _):
                i, j, done = carry
                valid = jnp.logical_not(done)
                cd = jnp.where((i > 0) & (j > 0), R[jnp.maximum(i - 1, 0), jnp.maximum(j - 1, 0)], BIG)
                cu = jnp.where(i > 0, R[jnp.maximum(i - 1, 0), j], BIG)
                cl = jnp.where(j > 0, R[i, jnp.maximum(j - 1, 0)], BIG)
                choice = jnp.argmin(jnp.stack([cd, cu, cl]))
                ni = jnp.where(choice <= 1, i - 1, i)
                nj = jnp.where((choice == 0) | (choice == 2), j - 1, j)
                at_origin = (i == 0) & (j == 0)
                ni = jnp.where(at_origin, 0, ni)
                nj = jnp.where(at_origin, 0, nj)
                return ((ni, nj, done | at_origin), (i, j, valid))
            init = (jnp.int32(T1 - 1), jnp.int32(T2 - 1), jnp.bool_(False))
            _, (i_idx, j_idx, valid) = lax.scan(step, init, None, length=L)
            return (i_idx, j_idx, valid)

        def _align_one(small, large):
            T_small, d = small.shape
            T_large = large.shape[0]
            D = _pairwise_euclidean(small, large)
            R = _dtw_cost(D)
            i_idx, j_idx, valid = _backtrack(R, T_small, T_large)
            contrib = small[i_idx] * valid[:, None].astype(small.dtype)
            expanded = jnp.zeros((T_large, d), dtype=small.dtype).at[j_idx].add(contrib)
            return expanded
        return jax.vmap(_align_one)(teacher_features, student_features)

    def _L0_ffn_ref(x, router_w, routing_bias, sw1, sw2, sw3, ew1, ew2, ew3):
        import jax, jax.numpy as jnp
        import numpy as np
        B, T, C, I, E = (4, 256, 128, 352, 7)

        def _swiglu(h, w1, w2, w3):
            return jax.nn.silu(h @ w1.T) * (h @ w3.T) @ w2.T
        b, t, c = x.shape
        shared_out = _swiglu(x, sw1, sw2, sw3)
        logits = jnp.clip(x @ router_w.T + routing_bias, -50.0, 50.0)
        probs = jax.nn.sigmoid(logits)
        num_switched = 1
        topk_probs, topk_idx = jax.lax.top_k(probs, num_switched)
        topk_probs = jnp.clip(topk_probs, 1e-08, 1.0 - 1e-08)
        xf = x.reshape(-1, c)
        sel = topk_idx.reshape(-1)
        p = topk_probs.reshape(-1)
        switched = jnp.zeros_like(xf)
        n_experts = ew1.shape[0]
        for e in range(n_experts):
            y = _swiglu(xf, ew1[e], ew2[e], ew3[e])
            w = jnp.where(sel == e, p, 0.0)
            switched = switched + w[:, None] * y
        switched = switched.reshape(b, t, c)
        total_weight = 0.5 + topk_probs.sum(axis=-1)
        total_weight = jnp.clip(total_weight[..., None] + 1e-08, 0.5, 2.0)
        return 0.5 / total_weight * shared_out + switched / total_weight
    x = x + _L0_attn_ref(_layernorm(x, axis=-1), L0_attn_W_in, L0_attn_b_in, L0_attn_W_s, L0_attn_b_s, L0_attn_W_o, L0_attn_b_o)
    x = x + _L0_xattn_ref(ctx_1024, _layernorm(x, axis=-1))
    x = x + _L0_ffn_ref(_layernorm(x, axis=-1), L0_ffn_router_w, L0_ffn_routing_bias, L0_ffn_sw1, L0_ffn_sw2, L0_ffn_sw3, L0_ffn_ew1, L0_ffn_ew2, L0_ffn_ew3)
    return x

_drawn_inputs = setup_inputs


def setup_inputs(seed=0):
    import zlib

    import numpy as np

    out = dict(_drawn_inputs(seed))
    spreads = {'L0_attn_b_in': (0.0, 0.8),
     'L0_attn_b_s': (0.0, 0.394),
     'L0_attn_b_o': (0.0, 0.1),
     'L0_ffn_routing_bias': (0.0, 0.1)}
    factors = {'L0_attn_W_in': 6.839, 'L0_attn_W_s': 6.043, 'L0_attn_W_o': 3.187}
    for name, (base, spread) in spreads.items():
        noise = np.random.default_rng([zlib.crc32(name.encode()), seed]).standard_normal(out[name].shape)
        drawn = base * np.exp(spread * noise) if base else spread * noise
        out[name] = jnp.asarray(drawn.astype(out[name].dtype))
    for name, factor in factors.items():
        out[name] = (out[name] * factor).astype(out[name].dtype)
    return out
```

```python
from contextlib import ExitStack

import numpy as np
import concourse.bass as bass
from concourse import mybir

F32 = mybir.dt.float32
F32R = mybir.dt.float32r
BF16 = mybir.dt.bfloat16
I32 = mybir.dt.int32
U32 = mybir.dt.uint32
ALU = mybir.AluOpType
ACT = mybir.ActivationFunctionType
AX_X = mybir.AxisListType.X

P = 128
NSEQ, T, D = 64, 64, 128
TOK = NSEQ * T
NT = TOK // P
CT = 4
NC = NT // CT
CW = CT * P
NE = 7
SH = NE
HID = 352
KC = 3
KW = [128, 128, HID - 256]
NS = (TOK - NE) // P + NE
ROW = D + 2
EPS = 1e-5
BIG = 1e30


class Track:

    def __init__(self, sem):
        self.sem, self.n = sem, 0

    def __call__(self, ins, by=1):
        self.n += by
        ins.then_inc(self.sem, by)
        return (self.sem, self.n)


def after(eng, *marks):
    for m in marks:
        if m is not None:
            eng.wait_ge(m[0], m[1])


def program(nc, x, ctx, ctxT, w_inT, b_in, w_sT, b_s, w_oT, b_o, router, r_bias, w13, w2, out, dbg=None):
    pe, dve, act, pool, sp = nc.tensor, nc.vector, nc.scalar, nc.gpsimd, nc.sync
    stack = ExitStack()
    with stack:
        def sem(name):
            return stack.enter_context(nc.semaphore(name))

        def sb(name, shape, dt=F32, at=stack):
            return at.enter_context(nc.sbuf_tensor(name, shape, dt))

        pe_done, dve_done, act_done, pool_done = (Track(sem(n)) for n in ("pe_done", "dve_done", "act_done", "pool_done"))
        bank = [stack.enter_context(nc.psum_tensor(f"bank{i}", [P, 512], F32)) for i in range(8)]

        def load(eng, dst, src, name):
            s = sem(name)
            eng.dma_start(dst, src).then_inc(s, 16)
            return (s, 16)

        def rows(ap):
            return ap.rearrange("b t d -> (b t) d").rearrange("(n p) d -> p n d", p=P)

        dist = nc.dram_tensor("dist", [NSEQ, T, T], F32, kind="Internal").ap()
        routed = nc.dram_tensor("routed", [NS * P, ROW], F32, kind="Internal").ap()

        xr = sb("xr", [P, NT, D])
        w13_hi = sb("w13_hi", [P, NE + 1, 2 * HID], F32R)
        w13_lo = sb("w13_lo", [P, NE + 1, 2 * HID], F32R)
        w2_hi = sb("w2_hi", [P, NE + 1, KC, D], F32R)
        w2_lo = sb("w2_lo", [P, NE + 1, KC, D], F32R)
        rt_hi = sb("rt_hi", [P, NE + 1], F32R)
        rt_lo = sb("rt_lo", [P, NE + 1], F32R)
        ident = sb("ident", [P, P])
        iota_i = sb("iota_i", [P, P], I32)
        iota_f = sb("iota_f", [P, P])
        half = sb("half", [P, NT])
        BNR = 4
        bn = sb("bn", [P, BNR, CT, 6])
        mvs = sb("mvs", [P, 3, NT, 2])
        ve = sb("ve", [P, 3, NT])
        rstds = sb("rstds", [P, 3, NT])

        x_in = [load(sp, xr[:, c * CT:(c + 1) * CT, :], rows(x)[:, c * CT:(c + 1) * CT, :], f"x_in{c}") for c in range(1)]

        cn = sb("cn", [P, NT, D])
        bounds = sb("bounds", [P, 2, NT])

        m = pool_done(pool.memset(ident[:, :], 0.0))
        after(pool, m)
        m_ident = pool_done(pool.affine_select(out=ident[:, :], in_=ident[:, :], compare_op=ALU.not_equal, fill=1.0,
                                               base=0, pattern=[[-1, P]], channel_multiplier=1))
        m = pool_done(pool.iota(iota_i[:, :], [[1, P]], base=0, channel_multiplier=0))
        after(pool, m)
        m_iota = pool_done(pool.tensor_copy(iota_f[:, :], iota_i[:, :]))
        m_half = pool_done(pool.memset(half[:, :], -0.5))

        rb = sb("rb", [P, NE])
        prio = sb("prio", [P, NE])
        prio_i = sb("prio_i", [P, NE], I32)
        tri = sb("tri", [P, P], BF16)
        ones = sb("ones", [P, P], BF16)
        onesf = sb("onesf", [P, NE])
        i128_i = sb("i128_i", [P, NT], I32)
        i128 = sb("i128", [P, NT])
        carry = sb("carry", [P, NE, NT])
        w_sh = sb("w_sh", [P, NT])
        pos_i = sb("pos_i", [P, NT], I32)
        ek_i = sb("ek_i", [1, NS], I32)
        fill = sb("fill", [P, ROW])
        m_rb = load(act, rb[:, :], r_bias.rearrange("(a e) -> a e", a=1).broadcast_to([P, NE]), "l_rb")
        m1 = pool_done(pool.iota(prio_i[:, :], [[-1, NE]], base=NE, channel_multiplier=0))
        m2 = pool_done(pool.iota(i128_i[:, :], [[P, NT]], base=0, channel_multiplier=0))
        after(pool, m1)
        pool_done(pool.tensor_copy(prio[:, :], prio_i[:, :]))
        after(pool, m2)
        pool_done(pool.tensor_copy(i128[:, :], i128_i[:, :]))
        pool_done(pool.memset(ones[:, :], 1.0))
        pool_done(pool.memset(onesf[:, :], 1.0))
        m1 = pool_done(pool.memset(tri[:, :], 1.0))
        m2 = pool_done(pool.memset(carry[:, :, :], 1.0))
        m3 = pool_done(pool.memset(fill[:, :], 0.0))
        after(pool, m1)
        pool_done(pool.affine_select(out=tri[:, :], in_=tri[:, :], compare_op=ALU.is_gt, fill=0.0,
                                     base=0, pattern=[[1, P]], channel_multiplier=-1))
        after(pool, m2)
        pool_done(pool.memset(carry[:, :, 0:1], 0.0))
        after(pool, m3)
        m_tri = pool_done(pool.memset(fill[:, ROW - 1:ROW].bitcast(I32), 1 << 20))
        after(act, m_tri)
        m_fill = load(act, routed.rearrange("(k p) r -> p k r", p=P), fill[:, None, :].to_broadcast([P, NS, ROW]), "fill_out")

        bn_read = []

        def ln_stats(k, c, src_ready):
            g = len(bn_read) % BNR
            after(dve, src_ready, bn_read[-BNR] if len(bn_read) >= BNR else None)
            marks = [dve_done(dve.bn_stats(bn[:, g, t, :], xr[:, c * CT + t, :])) for t in range(CT)]
            for t in range(CT):
                after(dve, marks[t])
                m = dve_done(dve.bn_aggr(mvs[:, k, c * CT + t, :], bn[:, g, t, :]))
            bn_read.append(m)
            s = slice(c * CT, (c + 1) * CT)
            after(pool, m, m_half)
            m2 = pool_done(pool.tensor_scalar(ve[:, k, s], mvs[:, k, s, 1], EPS, None, ALU.add))
            after(pool, m2)
            return pool_done(pool.tensor_tensor(rstds[:, k, s], ve[:, k, s], half[:, s], ALU.pow))

        def normalise(k, n, dst):
            return dve_done(dve.tensor_scalar(dst, xr[:, n, :], mvs[:, k, n, 0:1], rstds[:, k, n:n + 1], ALU.subtract, ALU.mult))

        with ExitStack() as st:
            w_in = sb("w_in", [P, 2 * D], at=st)
            w_s = sb("w_s", [P, D], at=st)
            w_o = sb("w_o", [P, D], at=st)
            bias = sb("bias", [P, 4], at=st)
            bo = sb("bo", [P, CT, D], at=st)
            cT = sb("cT", [P, TOK], at=st)
            aa = sb("aa", [P, NT], at=st)
            sq = sb("sq", [P, D], at=st)
            xn = sb("xn", [P, 2, CT, D], at=st)
            xnT = sb("xnT", [P, 2, CW], at=st)
            gate = sb("gate", [P, 2, CW], at=st)
            keep = sb("keep", [P, 2, CW], at=st)
            val = sb("val", [P, 2, CW], at=st)
            sv = sb("sv", [P, 2, CW], at=st)
            h = sb("h", [P, 2, CW], at=st)
            sn = sb("sn", [P, 2, CT, D], at=st)
            sT = sb("sT", [P, 2, CW], at=st)
            bb = sb("bb", [P, 2, CT], at=st)
            bbT = sb("bbT", [CT, 2, P], at=st)
            sel = sb("sel", [CT, CT, P], at=st)
            d2 = sb("d2", [P, 2, CT, T], at=st)

            m_w = [load(act, w_in[:, :], w_inT, "l_win"), load(act, bias[:, 0:2], b_in, "l_bin"),
                   load(act, w_s[:, :], w_sT, "l_ws"), load(act, bias[:, 2:3], b_s, "l_bs"),
                   load(act, w_o[:, :], w_oT, "l_wo")]
            m_bo = load(act, bo[:, :, :], b_o.rearrange("(a b d) -> a b d", a=1, b=1).broadcast_to([P, CT, D]), "l_bo")
            cn_in, cT_in = [], []
            for c in range(NC):
                s = slice(c * CT, (c + 1) * CT)
                if c:
                    x_in.append(load(sp, xr[:, s, :], rows(x)[:, s, :], f"x_in{c}"))
                cn_in.append(load(sp, cn[:, s, :], rows(ctx)[:, s, :], f"cn_in{c}"))
                cT_in.append(load(sp, cT[:, c * CW:(c + 1) * CW], ctxT[:, c * CW:(c + 1) * CW], f"cT_in{c}"))

            m = pool_done(pool.memset(sel[:, :, :], 0.0))
            after(pool, m)
            m_sel = pool_done(pool.affine_select(out=sel[:, :, :], in_=sel[:, :, :], compare_op=ALU.not_equal, fill=1.0,
                                                 base=0, pattern=[[-1, CT], [0, P]], channel_multiplier=1))
            after(act, m_w[1])
            m_nb = act_done(act.mul(bias[:, 3:4], bias[:, 0:1], -1.0))

            X_T, GATE, VAL, SV, OUT, S_T, BB, AB = bank
            hist = {}

            def old(name, c):
                return hist.get((name, c))

            def mark(name, c, m):
                hist[(name, c)] = m
                return m

            def chunk(c):
                b = c % 2
                s = slice(c * CT, (c + 1) * CT)
                m_st = ln_stats(0, c, x_in[c])
                yield
                after(dve, m_st, old("xnT", c - 2), old("xadd", c - 2))
                for t in range(CT):
                    m_xn = normalise(0, c * CT + t, xn[:, b, t, :])
                after(pe, m_xn, m_ident, old("xnT", c - 1))
                for t in range(CT):
                    m = pe_done(pe.transpose(X_T[:, t * P:(t + 1) * P], xn[:, b, t, :], ident[:, :]))
                yield
                after(act, m, old("VALp", c - 2))
                m_xT = mark("xnT", c, act_done(act.copy(xnT[:, b, :], X_T[:, :])))
                after(pe, m_xT, m_w[0], old("keep", c - 1))
                m_g = pe_done(pe.matmul(GATE[:, :], w_in[:, 0:D], xnT[:, b, :], start=True, stop=True))
                after(pe, old("val", c - 1))
                m_v = mark("VALp", c, pe_done(pe.matmul(VAL[:, :], w_in[:, D:2 * D], xnT[:, b, :], start=True, stop=True)))
                after(pool, m_bo, m_xn)
                m = pool_done(pool.tensor_tensor(xr[:, s, :], xr[:, s, :], bo[:, :, :], ALU.add))
                after(pool, m)
                mark("xadd", c, pool_done(pool.tensor_tensor(xr[:, s, :], xr[:, s, :], xn[:, b, :, :], ALU.add)))
                yield
                after(act, m_g, m_nb, m_w[3], old("scan", c - 2), old("b", c - 2))
                act_gate = act_done(act.activation(gate[:, b, :], GATE[:, :], ACT.Sigmoid, bias=bias[:, 0:1]))
                m_keep = mark("keep", c, act_done(act.activation(keep[:, b, :], GATE[:, :], ACT.Sigmoid, bias=bias[:, 3:4], scale=-1.0)))
                after(act, m_v, old("SVp", c - 2))
                m_val = mark("val", c, act_done(act.activation(val[:, b, :], VAL[:, :], ACT.Identity, bias=bias[:, 1:2])))
                after(pe, m_val, m_w[2], old("tanh", c - 1))
                m_s = mark("SVp", c, pe_done(pe.matmul(SV[:, :], w_s[:, :], val[:, b, :], start=True, stop=True)))
                yield
                after(pool, m_keep)
                m_reset = pool_done(pool.memset(keep[:, b, 0:CW:T], 0.0))
                after(act, m_s)
                m_tanh = mark("tanh", c, act_done(act.activation(sv[:, b, :], SV[:, :], ACT.Tanh, bias=bias[:, 2:3])))
                after(pool, m_tanh, act_gate)
                m_b = mark("b", c, pool_done(pool.tensor_tensor(sv[:, b, :], sv[:, b, :], gate[:, b, :], ALU.mult)))
                yield
                after(dve, m_b, m_reset, old("OUTp", c - 2))
                m_h = mark("scan", c, dve_done(dve.tensor_tensor_scan(h[:, b, :], keep[:, b, :], sv[:, b, :], 0.0, ALU.mult, ALU.add)))
                after(pe, m_h, m_w[4], old("x1", c - 1))
                for t in range(CT):
                    m = pe_done(pe.matmul(OUT[:, t * D:(t + 1) * D], h[:, b, t * P:(t + 1) * P], w_o[:, :], start=True, stop=True))
                m_o = mark("OUTp", c, m)
                yield
                after(dve, m_o, old("xadd", c))
                m_x1 = mark("x1", c, dve_done(dve.tensor_tensor(xr[:, s, :], OUT[:, :].rearrange("p (t d) -> p t d", d=D), xr[:, s, :], ALU.add)))
                m_st = ln_stats(1, c, m_x1)
                after(act, cn_in[c])
                for t in range(CT):
                    m_aa = act_done(act.activation(sq[:, :], cn[:, c * CT + t, :], ACT.Square, accum_out=aa[:, c * CT + t:c * CT + t + 1]))
                    after(act, m_aa)
                yield
                after(dve, m_st, old("sTt", c - 2))
                for t in range(CT):
                    m_sn = normalise(1, c * CT + t, sn[:, b, t, :])
                after(pool, m_st, old("bbt", c - 2))
                m = pool_done(pool.tensor_tensor(bb[:, b, :], rstds[:, 1, s], rstds[:, 1, s], ALU.mult))
                after(pool, m)
                m = pool_done(pool.tensor_tensor(bb[:, b, :], bb[:, b, :], mvs[:, 1, s, 1], ALU.mult))
                after(pool, m)
                m_bb = pool_done(pool.tensor_scalar(bb[:, b, :], bb[:, b, :], float(D), None, ALU.mult))
                after(pe, m_sn, m_ident, old("sT", c - 1))
                for t in range(CT):
                    m = pe_done(pe.transpose(S_T[:, t * P:(t + 1) * P], sn[:, b, t, :], ident[:, :]))
                m_t = mark("sTt", c, m)
                after(pe, m_bb, old("bbT", c - 1))
                m_bt = mark("bbt", c, pe_done(pe.transpose(BB[0:CT, 0:P], bb[:, b, :], ident[:, :])))
                yield
                after(act, m_t, old("ABp", c - 2))
                m_sT = mark("sT", c, act_done(act.mul(sT[:, b, :], S_T[:, :], -2.0)))
                after(act, m_bt)
                m_bT = mark("bbT", c, act_done(act.copy(bbT[:, b, :], BB[0:CT, 0:P])))
                after(pe, m_sT, m_bT, m_sel, cT_in[c], old("d2", c - 1))
                for t in range(CT):
                    a = slice(t * P, (t + 1) * P)
                    pe_done(pe.matmul(AB[:, a], cT[:, c * CW + t * P:c * CW + (t + 1) * P], sT[:, b, a], start=True, stop=False))
                    m = pe_done(pe.matmul(AB[:, a], sel[:, t, :], bbT[:, b, :], start=False, stop=True))
                m_ab = mark("ABp", c, m)
                yield
                after(dve, m_ab, m_aa, old("st0", c - 2), old("st1", c - 2))
                ab = AB[:, :].rearrange("p (t q j) -> p t q j", t=CT, q=2)
                for q in range(2):
                    r = slice(q * T, (q + 1) * T)
                    m = dve_done(dve.tensor_tensor(d2[r, b, :, :], ab[r, :, q, :], aa[r, s, None].to_broadcast([T, CT, T]), ALU.add))
                mark("d2", c, m)
                after(pool, m)
                m = pool_done(pool.tensor_scalar(d2[:, b, :, :], d2[:, b, :, :], 0.0, None, ALU.max))
                after(sp, m)
                for q in range(2):
                    seqs = dist[c * 2 * CT + q:(c + 1) * 2 * CT:2, :, :].rearrange("n i j -> i n j")
                    mark(f"st{q}", c, load(sp, seqs, d2[q * T:(q + 1) * T, b, :, :], f"dist{q}_{c}"))

            under_way, started = [], 0
            while under_way or started < NC:
                if started < NC:
                    under_way.append(chunk(started))
                    started += 1
                under_way = [g for g in under_way if next(g, "end") != "end"]

            m_dist = [hist[(f"st{q}", c)] for q in range(2) for c in range(NC)]
            stage1_end = [(t.sem, t.n) for t in (pe_done, dve_done, act_done, pool_done)]

        with ExitStack() as st:
            BR = 8
            NB = T // BR
            MR = 16
            Q = NSEQ
            dd = sb("dd", [Q, T, T], at=st)
            R = sb("R", [Q, T + 1, T + 1], at=st)
            mn = sb("mn", [Q, MR, T], at=st)
            q = sb("q", [Q, 2, BR, T], at=st)
            w = sb("w", [Q, T, T], BF16, at=st)
            left = sb("left", [Q, T, T + 1], BF16, at=st)
            v = sb("v", [Q, T, T + 1], BF16, at=st)
            F = sb("F", [Q, T, T + 1], BF16, at=st)
            dF = sb("dF", [Q, T, T], BF16, at=st)
            junk = sb("junk", [Q, T], BF16, at=st)
            W = sb("W", [Q, T + 1], at=st)
            Wd = sb("Wd", [Q, 2, 2, T], at=st)
            raw = sb("raw", [P, 2, 2 * HID + KC * D], at=st)
            rt_raw = sb("rt_raw", [P, NE + 1], at=st)

            after(sp, *m_dist, *stage1_end)
            blocks = [slice(0, 8), slice(8, 24), slice(24, 44), slice(44, 64)]
            dd_in = [load(sp, dd[:, r, :], dist[:, r, :], f"dd_in{k}") for k, r in enumerate(blocks)]
            for e in (pe, dve, act, pool):
                after(e, *stage1_end, *m_dist)

            pool_done(pool.memset(R[:, 0, :], BIG))
            pool_done(pool.memset(R[:, 1:, 0:1], BIG))
            pool_done(pool.memset(left[:, :, 0:1], 0.0))
            pool_done(pool.memset(v[:, :, 0:1], 0.0))
            pool_done(pool.memset(W[:, 0:1], 0.0))
            m_pads = pool_done(pool.memset(W[:, T:T + 1], float(T - 1)))

            m_dd = []
            for k, r in enumerate(blocks):
                after(act, dd_in[k])
                m_dd.append(act_done(act.activation(dd[:, r, :], dd[:, r, :], ACT.Sqrt)))
            row_dd = [m_dd[next(k for k, r in enumerate(blocks) if r.start <= i < r.stop)] for i in range(T)]

            raw_free = [None, None]
            m_split = []

            def split_weights(e):
                b = e % 2
                after(sp, raw_free[b])
                l1 = load(sp, raw[:, b, 0:2 * HID], w13[:, e, :], f"w13_in{e}")
                l2 = load(sp, raw[:, b, 2 * HID:], w2[:, e, :, :].rearrange("p k d -> p (k d)"), f"w2_in{e}")
                after(act, l1, l2)
                h1 = act_done(act.copy(w13_hi[:, e, :], raw[:, b, 0:2 * HID]))
                h2 = act_done(act.copy(w2_hi[:, e, :, :].rearrange("p k d -> p (k d)"), raw[:, b, 2 * HID:]))
                after(pool, h1)
                pool_done(pool.tensor_tensor(w13_lo[:, e, :], raw[:, b, 0:2 * HID], w13_hi[:, e, :].bitcast(F32), ALU.subtract))
                after(pool, h2)
                raw_free[b] = pool_done(pool.tensor_tensor(w2_lo[:, e, :, :].rearrange("p k d -> p (k d)"), raw[:, b, 2 * HID:],
                                                           w2_hi[:, e, :, :].rearrange("p k d -> p (k d)").bitcast(F32), ALU.subtract))
                m_split.append(raw_free[b])

            m_scan, m_min, m_left = [None] * T, [None] * T, [None] * T
            m_w, m_F, m_dF, m_v = [None] * NB, [None] * NB, [None] * NB, [None] * T

            def column_of(k):
                r = slice(k * BR, (k + 1) * BR)
                qb = q[:, k % 2, :, :]
                after(pool, m_scan[r.stop - 1], m_w[k - 2] if k >= 2 else m_pads)
                m = pool_done(pool.tensor_tensor(qb, R[:, r, 1:], R[:, r, 0:T], ALU.subtract))
                after(pool, m)
                m = pool_done(pool.tensor_scalar(qb, qb, 0.0, -0.5, ALU.is_ge, ALU.mult))
                after(pool, m, m_iota)
                m_w[k] = pool_done(pool.tensor_tensor(w[:, r, :], qb, iota_f[0:Q, None, 0:T].to_broadcast([Q, BR, T]), ALU.add))

            def choose(i):
                after(dve, m_left[i], m_w[i // BR])
                m_v[i] = dve_done(dve.scalar_tensor_tensor(v[:, i, 1:], left[:, i, 1:], 0.0, w[:, i, :], ALU.is_equal, ALU.mult))

            def spread(k):
                r = slice(k * BR, (k + 1) * BR)
                after(dve, m_v[r.stop - 1])
                flat = [a[:, r, :].rearrange("q i j -> q (i j)") for a in (F, left, v)]
                m_F[k] = dve_done(dve.tensor_tensor_scan(*flat, 0.0, ALU.mult, ALU.add))

            def steps(k):
                r = slice(k * BR, (k + 1) * BR)
                after(pool, m_F[k])
                m_dF[k] = pool_done(pool.tensor_tensor(dF[:, r, :], F[:, r, 1:], F[:, r, 0:T], ALU.subtract))

            LAG = 14
            after(dve, m_pads)
            for i in range(T + LAG):
                if i < T:
                    after(dve, m_scan[i - 1] if i else None, m_left[i - MR] if i >= MR else None)
                    m_min[i] = dve_done(dve.tensor_tensor(mn[:, i % MR, :], R[:, i, 1:], R[:, i, 0:T], ALU.min))
                if 1 <= i <= T:
                    after(dve, m_scan[i - 1], m_min[i - 1])
                    m_left[i - 1] = dve_done(dve.tensor_tensor(left[:, i - 1, 1:], R[:, i, 0:T], mn[:, (i - 1) % MR, :], ALU.is_lt))
                if i < T:
                    after(dve, m_min[i], row_dd[i])
                    m_scan[i] = dve_done(dve.tensor_tensor_scan(R[:, i + 1, 1:], mn[:, i % MR, :], dd[:, i, :],
                                                                BIG if i else 0.0, ALU.min, ALU.add))
                if i >= LAG:
                    choose(i - LAG)
                if i < T and i % BR == BR - 1:
                    column_of(i // BR)
                    split_weights(i // BR)
                if i >= LAG and (i - LAG) % BR == BR - 1:
                    spread((i - LAG) // BR)
                    steps((i - LAG) // BR)

            l = load(sp, rt_raw[:, :], router, "rt_in")
            after(act, l)
            m = act_done(act.copy(rt_hi[:, :], rt_raw[:, :]))
            after(pool, m)
            m_rt = pool_done(pool.tensor_tensor(rt_lo[:, :], rt_raw[:, :], rt_hi[:, :].bitcast(F32), ALU.subtract))

            m = None
            for i in range(T - 1, 0, -1):
                after(dve, m, m_dF[i // BR], m_iota, m_pads)
                m = dve_done(dve.scalar_tensor_tensor(junk[:, :], iota_f[0:Q, 0:T], W[:, i + 1:i + 2], dF[:, i, :], ALU.is_le, ALU.mult,
                                                      accum_out=W[:, i:i + 1]))
            after(dve, m)
            for k in range(2):
                m = dve_done(dve.tensor_copy(Wd[:, k, :, :], W[:, None, k:k + T].to_broadcast([Q, 2, T])))
            WT = bank[0]
            after(pe, m, m_ident)
            for k in range(2):
                m = pe_done(pe.transpose(WT[:, k * Q:(k + 1) * Q], Wd[:, k, :, :].rearrange("q a i -> q (a i)"), ident[0:Q, 0:Q]))
            after(dve, m)
            wt = WT[:, 0:2 * Q].rearrange("p (k n h) -> p k n h", k=2, h=2)
            dve_done(dve.tensor_copy(bounds[0:T, :, :], wt[0:T, :, :, 0]))
            m_bounds = dve_done(dve.tensor_scalar(bounds[T:P, :, :], wt[T:P, :, :, 1], float(T), None, ALU.add))
            stage2_end = [(t.sem, t.n) for t in (pe_done, dve_done, act_done, pool_done)]

        if True:
            st = stack
            mk = sb("mk", [P, 2, CT, P], at=st)
            xT_hi = sb("xT_hi", [P, TOK], F32R, at=st)
            xT_lo = sb("xT_lo", [P, TOK], F32R, at=st)
            pay = sb("pay", [P, NT, ROW], at=st)
            for e in (pe, dve, act, pool, sp):
                after(e, *stage2_end)
            m_id = pool_done(pool.iota(pay[:, :, D + 1:].bitcast(I32), [[P, NT], [1, 1]], base=0, channel_multiplier=1))
            ALIGN, X_T, LOGIT = bank[1], bank[7], bank[0]

            def aligned(c):
                b = c % 2
                s = slice(c * CT, (c + 1) * CT)
                after(dve, m_bounds, m_iota, old("al", c - 2))
                ms = [dve_done(dve.tensor_scalar(mk[:, b, t, :], iota_f[:, :], bounds[:, 1, c * CT + t:c * CT + t + 1], None, ALU.is_le))
                      for t in range(CT)]
                for t in range(CT):
                    n = c * CT + t
                    after(dve, ms[t])
                    m_mk = dve_done(dve.scalar_tensor_tensor(mk[:, b, t, :], iota_f[:, :], bounds[:, 0, n:n + 1], mk[:, b, t, :], ALU.is_ge, ALU.mult))
                after(pe, m_mk, old("x2", c - 1))
                for t in range(CT):
                    m = pe_done(pe.matmul(ALIGN[:, t * D:(t + 1) * D], mk[:, b, t, :], cn[:, c * CT + t, :], start=True, stop=True))
                mark("al", c, m)
                yield
                after(dve, m)
                m_x2 = mark("x2", c, dve_done(dve.tensor_tensor(xr[:, s, :], ALIGN[:, :].rearrange("p (t d) -> p t d", d=D), xr[:, s, :], ALU.add)))
                m_st = ln_stats(2, c, m_x2)
                yield
                after(dve, m_st)
                for t in range(CT):
                    m_n = normalise(2, c * CT + t, pay[:, c * CT + t, 0:D])
                after(pe, m_n, old("xT_lo", c - 1))
                for t in range(CT):
                    m = pe_done(pe.transpose(X_T[:, t * P:(t + 1) * P], pay[:, c * CT + t, 0:D], ident[:, :]))
                yield
                a = slice(c * CW, (c + 1) * CW)
                after(act, m)
                m_hi = mark("xT_hi", c, act_done(act.copy(xT_hi[:, a], X_T[:, :])))
                after(dve, m_hi)
                m_lo = mark("xT_lo", c, dve_done(dve.tensor_tensor(xT_lo[:, a], X_T[:, :], xT_hi[:, a].bitcast(F32), ALU.subtract)))
                after(pe, m_lo, m_hi, m_rt)
                for t in range(CT):
                    n = c * CT + t
                    r = slice(n * P, (n + 1) * P)
                    o = LOGIT[:, n * (NE + 1):(n + 1) * (NE + 1)]
                    pe.matmul(o, xT_hi[:, r], rt_hi[:, :], start=True, stop=False)
                    pe.matmul(o, xT_hi[:, r], rt_lo[:, :], start=False, stop=False)
                    m = pe_done(pe.matmul(o, xT_lo[:, r], rt_hi[:, :], start=False, stop=True))
                mark("logit", c, m)

            under_way, started = [], 0
            while under_way or started < NC:
                if started < NC:
                    under_way.append(aligned(started))
                    started += 1
                under_way = [g for g in under_way if next(g, "end") != "end"]

        with ExitStack() as st:
            def e8(name, dt=F32):
                return sb(name, [P, NT, NE], dt, at=st)
            lg, pr, oh, key, t1 = (e8(n) for n in ("lg", "pr", "oh", "key", "t1"))
            oh_b = e8("oh_b", BF16)
            cnt, incl, base, lt = (sb(n, [P, NE, NT], at=st) for n in ("cnt", "incl", "base", "lt"))
            pm, km, sc, inv, pos = (sb(n, [P, NT], at=st) for n in ("pm", "km", "sc", "inv", "pos"))
            te, ends = (sb(n, [P, NE], at=st) for n in ("te", "ends"))
            ekc = sb("ekc", [1, NS, NE - 1], at=st)
            ekf = sb("ekf", [1, NS], at=st)
            RANK, COUNT = bank[1], bank[6]

            after(dve, old("logit", NC - 1), m_rb)
            lgp = LOGIT[:, 0:NT * (NE + 1)].rearrange("p (n e) -> p n e", e=NE + 1)[:, :, 0:NE]

            def chain(ins):
                m = dve_done(ins)
                after(dve, m)
                return m

            def over_e(a):
                return a[:, :, None].to_broadcast([P, NT, NE])

            chain(dve.tensor_tensor(lg[:, :, :], lgp, rb[:, None, :].to_broadcast([P, NT, NE]), ALU.add))
            m = chain(dve.tensor_scalar(lg[:, :, :], lg[:, :, :], -50.0, 50.0, ALU.max, ALU.min))
            after(act, m)
            m = act_done(act.activation(pr[:, :, :], lg[:, :, :], ACT.Sigmoid))
            after(dve, m)
            chain(dve.tensor_reduce(pm[:, :], pr[:, :, :], AX_X, ALU.max))
            chain(dve.tensor_tensor(oh[:, :, :], pr[:, :, :], over_e(pm), ALU.is_equal))
            chain(dve.tensor_tensor(key[:, :, :], oh[:, :, :], prio[:, None, :].to_broadcast([P, NT, NE]), ALU.mult))
            chain(dve.tensor_reduce(km[:, :], key[:, :, :], AX_X, ALU.max))
            m_oh = chain(dve.tensor_tensor(oh_b[:, :, :], key[:, :, :], over_e(km), ALU.is_equal))
            ohf = oh_b[:, :, :].rearrange("p n e -> p (n e)")
            after(pe, m_oh, m_tri)
            m_rank = pe_done(pe.matmul(RANK[:, 0:NT * NE], tri[:, :], ohf, start=True, stop=True))
            m_cnt = pe_done(pe.matmul(COUNT[:, 0:NT * NE], ones[:, :], ohf, start=True, stop=True))
            chain(dve.tensor_scalar(pm[:, :], pm[:, :], 1e-8, 1.0 - 1e-8, ALU.max, ALU.min))
            chain(dve.tensor_scalar(sc[:, :], pm[:, :], 0.5, 1e-8, ALU.add, ALU.add))
            chain(dve.tensor_scalar(sc[:, :], sc[:, :], 0.5, 2.0, ALU.max, ALU.min))
            chain(dve.reciprocal(inv[:, :], sc[:, :]))
            chain(dve.tensor_tensor(pay[:, :, D], pm[:, :], inv[:, :], ALU.mult))
            m_ws = chain(dve.tensor_scalar(w_sh[:, :], inv[:, :], 0.5, None, ALU.mult))
            after(dve, m_cnt)
            chain(dve.tensor_copy(cnt[:, :, :], COUNT[:, 0:NT * NE].rearrange("p (n e) -> p e n", e=NE)))
            chain(dve.tensor_tensor_scan(incl[:, :, :].rearrange("p e n -> p (e n)"), carry[:, :, :].rearrange("p e n -> p (e n)"),
                                         cnt[:, :, :].rearrange("p e n -> p (e n)"), 0.0, ALU.mult, ALU.add))
            chain(dve.tensor_tensor(lt[:, :, :], i128[:, None, 0:NT].to_broadcast([P, NE, NT]),
                                    incl[:, :, NT - 1:NT].to_broadcast([P, NE, NT]), ALU.is_lt))
            chain(dve.tensor_reduce(te[:, :], lt[:, :, :], AX_X, ALU.add))
            m_ends = chain(dve.tensor_tensor_scan(ends[:, :], onesf[:, 0:NE], te[:, :], 0.0, ALU.mult, ALU.add))
            chain(dve.tensor_tensor(te[:, :], ends[:, :], te[:, :], ALU.subtract))
            chain(dve.tensor_tensor(base[:, :, :], incl[:, :, :], cnt[:, :, :], ALU.subtract))
            chain(dve.scalar_tensor_tensor(base[:, :, :], te[:, :, None].to_broadcast([P, NE, NT]), float(P), base[:, :, :], ALU.mult, ALU.add))
            after(dve, m_rank)
            chain(dve.tensor_tensor(t1[:, :, :], RANK[:, 0:NT * NE].rearrange("p (n e) -> p n e", e=NE),
                                    base[:, :, :].rearrange("p e n -> p n e"), ALU.add))
            chain(dve.tensor_tensor(t1[:, :, :], t1[:, :, :], oh_b[:, :, :], ALU.mult))
            chain(dve.tensor_reduce(pos[:, :], t1[:, :, :], AX_X, ALU.add))
            m_pos = chain(dve.tensor_copy(pos_i[:, :], pos[:, :]))
            chain(dve.tensor_tensor(ekc[:, :, :], ends[0:1, None, 0:NE - 1].to_broadcast([1, NS, NE - 1]),
                                    iota_f[0:1, 0:NS, None].to_broadcast([1, NS, NE - 1]), ALU.is_le))
            chain(dve.tensor_reduce(ekf[:, :], ekc[:, :, :], AX_X, ALU.add))
            m_ek = chain(dve.tensor_copy(ek_i[:, :], ekf[:, :]))
            router_end = [(t.sem, t.n) for t in (pe_done, dve_done, act_done)]

        s_put = sem("s_put")
        after(pool, m_pos, m_fill, m_id)
        for n in range(NT):
            pool.indirect_dma_start(routed, bass.IndirectOffsetOnAxis(ap=pos_i[:, n:n + 1], axis=0), pay[:, n, :], None,
                                    bounds_check=NS * P - 1).then_inc(s_put, 16)
        m_put = (s_put, NT * 16)

        for e in (pe, dve, act):
            after(e, *router_end)
        xs = sb("xs", [P, NS, ROW])
        spare = cn[:, :, :].rearrange("p n d -> p (n d)")

        def take(at, *shape):
            n = int(np.prod(shape))
            names = "abc"[:len(shape)]
            return spare[:, at:at + n].rearrange(f"p ({' '.join(names)}) -> p {' '.join(names)}", **dict(zip(names, shape)))

        g = take(0, 2, CW)
        h32 = take(2 * CW, 2, CW)
        yt = take(4 * CW, 2, CT, D)
        y = take(6 * CW, 2, D)
        h_hi = sb("h_hi", [P, 2, KC, CW], F32R)
        h_lo = sb("h_lo", [P, 2, KC, CW], F32R)
        xs_hi = sb("xs_hi", [P, 2, P], F32R)
        xs_lo = sb("xs_lo", [P, 2, P], F32R)

        after(sp, m_put, *router_end)
        m_xs = load(sp, xs[:, :, :], routed.rearrange("(k p) r -> p k r", p=P), "xs_in")

        A, U, Y, HT = bank[2:5:2], bank[3:6:2], bank[6], bank[0:2]
        free = {}

        def three(o, lhs, rhs):
            (lh, ll), (rh, rl) = lhs, rhs
            return [(o, lh, rh), (o, lh, rl), (o, ll, rh)]

        def products(ps):
            for k, (o, l, r) in enumerate(ps):
                ins = pe.matmul(o, l, r, start=(k == 0), stop=(k == len(ps) - 1))
            return ins

        def shared(c):
            b = c % 2
            a = slice(c * CW, (c + 1) * CW)
            xT = (xT_hi[:, a], xT_lo[:, a])
            for k in range(KC):
                kw, i = KW[k], (c * KC + k) % 2
                after(pe, m_split[SH], free.get(("U", i)), old("xT_lo", c))
                wa = slice(k * P, k * P + kw)
                wu = slice(HID + k * P, HID + k * P + kw)
                m_a = pe_done(products(three(A[i][0:kw, :], (w13_hi[:, SH, wa], w13_lo[:, SH, wa]), xT)))
                m_u = pe_done(products(three(U[i][0:kw, :], (w13_hi[:, SH, wu], w13_lo[:, SH, wu]), xT)))
                after(act, m_a, free.get(("g", i)))
                m_g = act_done(act.activation(g[0:kw, i, :], A[i][0:kw, :], ACT.Silu))
                after(dve, m_g, m_u, free.get(("h32", i)))
                m = free[("U", i)] = free[("g", i)] = dve_done(dve.tensor_tensor(h32[0:kw, i, :], U[i][0:kw, :], g[0:kw, i, :], ALU.mult))
                after(act, m, free.get(("h", b)) if k == 0 else None)
                m_hi = act_done(act.copy(h_hi[0:kw, b, k, :], h32[0:kw, i, :]))
                after(dve, m_hi)
                m_lo = free[("h32", i)] = dve_done(dve.tensor_tensor(h_lo[0:kw, b, k, :], h32[0:kw, i, :], h_hi[0:kw, b, k, :].bitcast(F32), ALU.subtract))
            return m_lo

        def shared_down(c, m_lo):
            b = c % 2
            after(pe, m_lo, free.get("Y"))
            for t in range(CT):
                r = slice(t * P, (t + 1) * P)
                ps = []
                for k in range(KC):
                    kw = KW[k]
                    ps += three(Y[:, t * D:(t + 1) * D], (h_hi[0:kw, b, k, r], h_lo[0:kw, b, k, r]), (w2_hi[0:kw, SH, k, :], w2_lo[0:kw, SH, k, :]))
                m = pe_done(products(ps))
            free[("h", b)] = m
            after(dve, m, m_ws)
            for t in range(CT):
                n = c * CT + t
                m = dve_done(dve.scalar_tensor_tensor(xr[:, n, :], Y[:, t * D:(t + 1) * D], w_sh[:, n:n + 1], xr[:, n, :], ALU.mult, ALU.add))
            free["Y"] = mark("x3", c, m)

        BEFORE = 6
        for c in range(BEFORE):
            m_lo = shared(c)
            if c:
                shared_down(c - 1, m_prev)
            m_prev = m_lo
        shared_down(BEFORE - 1, m_prev)

        all_end = [(t.sem, t.n) for t in (pe_done, dve_done, act_done)]
        for e in (pe, dve, act):
            after(e, *all_end)
        s_x, s_xh, s_xl, s_a, s_u, s_g, s_h, s_t, s_hh, s_hl, s_y, s_ys = (sem("tile_" + n) for n in
            ("x", "x_hi", "x_lo", "a", "u", "silu", "h", "hT", "hT_hi", "hT_lo", "y", "y_out"))
        s_o = [sem("tile_put0"), sem("tile_put1")]
        hT_hi = h_hi[:, :, :, 0:P]
        hT_lo = h_lo[:, :, :, 0:P]
        X = bank[7]
        ytok = nc.dram_tensor("ytok", [TOK, D], F32, kind="Internal").ap()

        def x_pe(k, i, first=False):
            after(pe, m_xs)
            if not first:
                pe.wait_ge(s_xl, k)
            pe.transpose(X[:, 0:P], slot(k, 0, D), ident[:, :]).then_inc(s_x, 1)

        xs_flat = xs[:, :, :].rearrange("p k r -> p (k r)")

        def cols(start, n):
            return slice(start, start + n) if isinstance(start, int) else bass.ds(start, n)

        def slot(k, first, n):
            return xs_flat[:, cols(k * ROW + first, n)]

        def routed_step(s, i, do):
            j = 1 - i
            if "up" in do:
                ex = pe.value_load(ek_i[0:1, cols(s, 1)], min_val=0, max_val=NE - 1)
                pe.wait_ge(s_xl, s + 1)
                if "again" in do:
                    pe.wait_ge(s_h, s - 1)
                xT = (xs_hi[:, i, :], xs_lo[:, i, :])
                for o, off, sg in ((A[i], 0, s_a), (U[i], HID, s_u)):
                    hi = w13_flat_hi[:, bass.ds(ex * (2 * HID) + off, HID)]
                    lo = w13_flat_lo[:, bass.ds(ex * (2 * HID) + off, HID)]
                    products(three(o[:, 0:HID], xT, (hi, lo))).then_inc(sg, 1)
                act.wait_ge(s_a, s + 1)
                if "again" in do:
                    act.wait_ge(s_t, s - 1)
                act.activation(g[:, i, 0:HID], A[i][:, 0:HID], ACT.Silu).then_inc(s_g, 1)
                dve.wait_ge(s_u, s + 1)
                dve.wait_ge(s_g, s + 1)
                dve.tensor_tensor(g[:, i, 0:HID], U[i][:, 0:HID], g[:, i, 0:HID], ALU.mult).then_inc(s_h, 1)
            if "turn" in do:
                pe.wait_ge(s_h, s)
                if "turn again" in do:
                    pe.wait_ge(s_hl, s - 2)
                for k in range(KC):
                    ins = pe.transpose(HT[j][0:KW[k], k * P:(k + 1) * P], g[:, j, k * P:k * P + KW[k]], ident[:, :])
                ins.then_inc(s_t, 1)
            if "down" in do:
                ex2 = pe.value_load(ek_i[0:1, cols(s - 2, 1)], min_val=0, max_val=NE - 1)
                pe.wait_ge(s_hl, s - 1)
                if "down again" in do:
                    pe.wait_ge(s_ys, s - 2)
                ps = []
                for k in range(KC):
                    kw = KW[k]
                    hi = w2_flat_hi[0:kw, bass.ds(ex2 * (KC * D) + k * D, D)]
                    lo = w2_flat_lo[0:kw, bass.ds(ex2 * (KC * D) + k * D, D)]
                    ps += three(Y[:, 0:D], (h_hi[0:kw, i, k, 0:P], h_lo[0:kw, i, k, 0:P]), (hi, lo))
                products(ps).then_inc(s_y, 1)
            if "x" in do:
                x_pe(s + 1, j)
            if "turn" in do:
                act.wait_ge(s_t, s)
                if "turn again" in do:
                    act.wait_ge(s_y, s - 2)
                act.copy(h_hi[:, j, 0:2, 0:P], HT[j][:, 0:2 * P].rearrange("p (k t) -> p k t", k=2)).then_inc(s_hh, 1)
                act.copy(h_hi[0:KW[2], j, 2, 0:P], HT[j][0:KW[2], 2 * P:3 * P]).then_inc(s_hh, 1)
                dve.wait_ge(s_hh, 2 * s)
                dve.tensor_tensor(h_lo[:, j, 0:2, 0:P], HT[j][:, 0:2 * P].rearrange("p (k t) -> p k t", k=2),
                                  h_hi[:, j, 0:2, 0:P].bitcast(F32), ALU.subtract)
                dve.tensor_tensor(h_lo[0:KW[2], j, 2, 0:P], HT[j][0:KW[2], 2 * P:3 * P],
                                  h_hi[0:KW[2], j, 2, 0:P].bitcast(F32), ALU.subtract).then_inc(s_hl, 1)
            if "x" in do:
                x_split(s + 1, j, "again x" in do)
            if "down" in do:
                dve.wait_ge(s_y, s - 1)
                if "put again" in do:
                    dve.wait_ge(s_o[i], 16 * half_of(s - 2))
                dve.tensor_scalar(y[:, i, :], Y[:, 0:D], slot(s - 2, D, 1), None, ALU.mult).then_inc(s_ys, 1)
                pool.wait_ge(s_ys, s - 1)
                pool.indirect_dma_start(ytok, bass.IndirectOffsetOnAxis(ap=slot(s - 2, D + 1, 1).bitcast(U32), axis=0),
                                        y[:, i, :], None, bounds_check=TOK - 1, oob_is_err=False).then_inc(s_o[i], 16)

        def half_of(k):
            return k // 2

        def x_split(k, i, again):
            act.wait_ge(s_x, k + 1)
            if again:
                act.wait_ge(s_u, k - 1)
            act.copy(xs_hi[:, i, :], X[:, 0:P]).then_inc(s_xh, 1)
            dve.wait_ge(s_xh, k + 1)
            dve.tensor_tensor(xs_lo[:, i, :], X[:, 0:P], xs_hi[:, i, :].bitcast(F32), ALU.subtract).then_inc(s_xl, 1)

        w13_flat_hi = w13_hi[:, :, :].rearrange("p e h -> p (e h)")
        w13_flat_lo = w13_lo[:, :, :].rearrange("p e h -> p (e h)")
        w2_flat_hi = w2_hi[:, :, :, :].rearrange("p e k d -> p (e k d)")
        w2_flat_lo = w2_lo[:, :, :, :].rearrange("p e k d -> p (e k d)")

        after(dve, m_xs)
        x_pe(0, 0, first=True)
        x_split(0, 0, False)
        for s in range(NS + 2):
            do = set()
            if s < NS:
                do.add("up")
                if s >= 2:
                    do.add("again")
            if s >= 1 and s <= NS:
                do.add("turn")
                if s >= 3:
                    do.add("turn again")
            if s >= 2:
                do.add("down")
                if s >= 3:
                    do.add("down again")
                if s >= 4:
                    do.add("put again")
            if s + 1 < NS:
                do.add("x")
                if s + 1 >= 2:
                    do.add("again x")
            routed_step(s, s % 2, do)

        for c in range(BEFORE, NC):
            m_lo = shared(c)
            shared_down(c, m_lo)
        m_y = [(s_o[0], 16 * (NS // 2)), (s_o[1], 16 * (NS // 2))]
        after(sp, *m_y)
        order = list(range(NC))
        yt_in = {}
        for q, c in enumerate(order):
            s = slice(c * CT, (c + 1) * CT)
            b = q % 2
            after(sp, free.get(("yt", b)))
            l = load(sp, yt[:, b, :, :], ytok.rearrange("(n p) d -> p n d", p=P)[:, s, :], f"y_in{c}")
            after(dve, l, old("x3", c))
            m = free[("yt", b)] = dve_done(dve.tensor_tensor(xr[:, s, :], xr[:, s, :], yt[:, b, :, :], ALU.add))
            after(sp, m)
            mark("out", c, load(sp, rows(out)[:, s, :], xr[:, s, :], f"out{c}"))
        after(sp, *(old("out", c) for c in range(NC)))


_OUTS = [((64, 64, 128), "float32")]


def kernel(**inputs):
    import numpy as _np
    import concourse.bacc as _bacc
    from concourse import mybir as _mybir
    from concourse.bass_utils import run_bass_kernel_spmd as _run

    g = {k.replace("L0_", ""): _np.asarray(v) for k, v in inputs.items()}
    w1 = _np.concatenate([g["ffn_ew1"], g["ffn_sw1"][None]])
    w3 = _np.concatenate([g["ffn_ew3"], g["ffn_sw3"][None]])
    w2 = _np.concatenate([g["ffn_ew2"], g["ffn_sw2"][None]])
    w13 = _np.concatenate([w1, w3], axis=1).transpose(2, 0, 1)
    w2p = _np.zeros((NE + 1, D, KC * P), w2.dtype)
    w2p[:, :, :HID] = w2
    w2p = w2p.reshape(NE + 1, D, KC, P).transpose(3, 0, 2, 1)
    rt = _np.zeros((D, NE + 1), g["ffn_router_w"].dtype)
    rt[:, :NE] = g["ffn_router_w"].T
    args_np = {
        "x": g["x"], "ctx": g["ctx_1024"], "ctxT": g["ctx_1024"].reshape(TOK, D).T,
        "w_inT": g["attn_W_in"].T, "b_in": g["attn_b_in"].reshape(2, D).T, "w_sT": g["attn_W_s"].T, "b_s": g["attn_b_s"].reshape(1, D).T,
        "w_oT": g["attn_W_o"].T, "b_o": g["attn_b_o"], "router": rt, "r_bias": g["ffn_routing_bias"],
        "w13": w13, "w2": w2p,
    }
    nc = _bacc.Bacc("TRN2", target_bir_lowering=False, num_devices=1)
    arrays, args = {}, []
    for name, a in args_np.items():
        a = _np.ascontiguousarray(a)
        arrays[f"in_{name}"] = a
        args.append(nc.dram_tensor(f"in_{name}", a.shape, _mybir.dt.from_np(a.dtype), kind="ExternalInput").ap())
    args.append(nc.dram_tensor("out_0", (64, 64, 128), _mybir.dt.float32, kind="ExternalOutput").ap())
    program(nc, *args)
    r = _run(nc, [arrays], core_ids=[0])
    return r.results[0]["out_0"]
```

```python
from contextlib import ExitStack

import numpy as np
import concourse.bass as bass
from concourse import mybir

F32 = mybir.dt.float32
F32R = mybir.dt.float32r
BF16 = mybir.dt.bfloat16
I32 = mybir.dt.int32
U32 = mybir.dt.uint32
ALU = mybir.AluOpType
ACT = mybir.ActivationFunctionType
AX_X = mybir.AxisListType.X

P = 128
NSEQ, T, D = 64, 64, 128
TOK = NSEQ * T
NT = TOK // P
CT = 4
NC = NT // CT
CW = CT * P
NE = 7
SH = NE
HID = 352
KC = 3
KW = [128, 128, HID - 256]
NS = (TOK - NE) // P + NE
NB4 = (NS + 2) // 4
ROW = D + 2
EPS = 1e-5
BIG = 1e30


class Track:

    def __init__(self, sem):
        self.sem, self.n = sem, 0

    def __call__(self, ins, by=1):
        self.n += by
        ins.then_inc(self.sem, by)
        return (self.sem, self.n)


def after(eng, *marks):
    for m in marks:
        if m is not None:
            eng.wait_ge(m[0], m[1])


def program(nc, x, ctx, ctxT, w_inT, b_in, w_sT, b_s, w_oT, b_o, router, r_bias, w13, w2, out, dbg=None):
    pe, dve, act, pool, sp = nc.tensor, nc.vector, nc.scalar, nc.gpsimd, nc.sync
    stack = ExitStack()
    with stack:
        def sem(name):
            return stack.enter_context(nc.semaphore(name))

        def sb(name, shape, dt=F32, at=stack):
            return at.enter_context(nc.sbuf_tensor(name, shape, dt))

        pe_done, dve_done, act_done, pool_done = (Track(sem(n)) for n in ("pe_done", "dve_done", "act_done", "pool_done"))
        bank = [stack.enter_context(nc.psum_tensor(f"bank{i}", [P, 512], F32)) for i in range(8)]

        def load(eng, dst, src, name):
            s = sem(name)
            eng.dma_start(dst, src).then_inc(s, 16)
            return (s, 16)

        def rows(ap):
            return ap.rearrange("b t d -> (b t) d").rearrange("(n p) d -> p n d", p=P)

        dist = nc.dram_tensor("dist", [NSEQ, T, T], F32, kind="Internal").ap()
        routed = nc.dram_tensor("routed", [NS * P, ROW], F32, kind="Internal").ap()

        xr = sb("xr", [P, NT, D])
        w13_hi = sb("w13_hi", [P, NE + 1, 2 * HID], F32R)
        w13_lo = sb("w13_lo", [P, NE + 1, 2 * HID], F32R)
        w2_2 = sb("w2_2", [P, NE + 1, KC, 2, D], F32R)
        rt_hi = sb("rt_hi", [P, NE + 1], F32R)
        rt_lo = sb("rt_lo", [P, NE + 1], F32R)
        ident = sb("ident", [P, P])
        iota_i = sb("iota_i", [P, P], I32)
        iota_f = sb("iota_f", [P, P])
        half = sb("half", [P, NT])
        BNR = 4
        bn = sb("bn", [P, BNR, CT, 6])
        mvs = sb("mvs", [P, 3, NT, 2])
        ve = sb("ve", [P, 3, NT])
        rstds = sb("rstds", [P, 3, NT])

        x_in = [load(sp, xr[:, c * CT:(c + 1) * CT, :], rows(x)[:, c * CT:(c + 1) * CT, :], f"x_in{c}") for c in range(1)]

        cn = sb("cn", [P, NT, D])
        bounds = sb("bounds", [P, 2, NT])

        m = pool_done(pool.memset(ident[:, :], 0.0))
        after(pool, m)
        m_ident = pool_done(pool.affine_select(out=ident[:, :], in_=ident[:, :], compare_op=ALU.not_equal, fill=1.0,
                                               base=0, pattern=[[-1, P]], channel_multiplier=1))
        m = pool_done(pool.iota(iota_i[:, :], [[1, P]], base=0, channel_multiplier=0))
        after(pool, m)
        m_iota = pool_done(pool.tensor_copy(iota_f[:, :], iota_i[:, :]))
        m_half = pool_done(pool.memset(half[:, :], -0.5))

        rb = sb("rb", [P, NE])
        prio = sb("prio", [P, NE])
        prio_i = sb("prio_i", [P, NE], I32)
        tri = sb("tri", [P, P], BF16)
        ones = sb("ones", [P, P], BF16)
        onesf = sb("onesf", [P, NE])
        i128_i = sb("i128_i", [P, NT], I32)
        i128 = sb("i128", [P, NT])
        carry = sb("carry", [P, NE, NT])
        w_sh = sb("w_sh", [P, NT])
        pos_i = sb("pos_i", [P, NT], I32)
        up_at = sb("up_at", [1, NB4 * 4 + 4], I32)
        down_at = sb("down_at", [1, NB4 * 4], I32)
        fill = sb("fill", [P, ROW])
        m_rb = load(act, rb[:, :], r_bias.rearrange("(a e) -> a e", a=1).broadcast_to([P, NE]), "l_rb")
        m1 = pool_done(pool.iota(prio_i[:, :], [[-1, NE]], base=NE, channel_multiplier=0))
        m2 = pool_done(pool.iota(i128_i[:, :], [[P, NT]], base=0, channel_multiplier=0))
        after(pool, m1)
        pool_done(pool.tensor_copy(prio[:, :], prio_i[:, :]))
        after(pool, m2)
        pool_done(pool.tensor_copy(i128[:, :], i128_i[:, :]))
        pool_done(pool.memset(ones[:, :], 1.0))
        pool_done(pool.memset(onesf[:, :], 1.0))
        pool_done(pool.memset(up_at[:, :], 0))
        pool_done(pool.memset(down_at[:, :], 0))
        m1 = pool_done(pool.memset(tri[:, :], 1.0))
        m2 = pool_done(pool.memset(carry[:, :, :], 1.0))
        m3 = pool_done(pool.memset(fill[:, :], 0.0))
        after(pool, m1)
        pool_done(pool.affine_select(out=tri[:, :], in_=tri[:, :], compare_op=ALU.is_gt, fill=0.0,
                                     base=0, pattern=[[1, P]], channel_multiplier=-1))
        after(pool, m2)
        pool_done(pool.memset(carry[:, :, 0:1], 0.0))
        after(pool, m3)
        m_tri = pool_done(pool.memset(fill[:, ROW - 1:ROW].bitcast(I32), 1 << 20))
        after(act, m_tri)
        m_fill = load(act, routed.rearrange("(k p) r -> p k r", p=P), fill[:, None, :].to_broadcast([P, NS, ROW]), "fill_out")

        bn_read = []

        def ln_stats(k, c, src_ready):
            g = len(bn_read) % BNR
            after(dve, src_ready, bn_read[-BNR] if len(bn_read) >= BNR else None)
            marks = [dve_done(dve.bn_stats(bn[:, g, t, :], xr[:, c * CT + t, :])) for t in range(CT)]
            for t in range(CT):
                after(dve, marks[t])
                m = dve_done(dve.bn_aggr(mvs[:, k, c * CT + t, :], bn[:, g, t, :]))
            bn_read.append(m)
            s = slice(c * CT, (c + 1) * CT)
            after(pool, m, m_half)
            m2 = pool_done(pool.tensor_scalar(ve[:, k, s], mvs[:, k, s, 1], EPS, None, ALU.add))
            after(pool, m2)
            return pool_done(pool.tensor_tensor(rstds[:, k, s], ve[:, k, s], half[:, s], ALU.pow))

        def normalise(k, n, dst):
            return dve_done(dve.tensor_scalar(dst, xr[:, n, :], mvs[:, k, n, 0:1], rstds[:, k, n:n + 1], ALU.subtract, ALU.mult))

        with ExitStack() as st:
            w_in = sb("w_in", [P, 2 * D], at=st)
            w_s = sb("w_s", [P, D], at=st)
            w_o = sb("w_o", [P, D], at=st)
            bias = sb("bias", [P, 4], at=st)
            bo = sb("bo", [P, CT, D], at=st)
            cT = sb("cT", [P, TOK], at=st)
            aa = sb("aa", [P, NT], at=st)
            sq = sb("sq", [P, D], at=st)
            xn = sb("xn", [P, 2, CT, D], at=st)
            xnT = sb("xnT", [P, 2, CW], at=st)
            gate = sb("gate", [P, 2, CW], at=st)
            keep = sb("keep", [P, 2, CW], at=st)
            val = sb("val", [P, 2, CW], at=st)
            sv = sb("sv", [P, 2, CW], at=st)
            h = sb("h", [P, 2, CW], at=st)
            sn = sb("sn", [P, 2, CT, D], at=st)
            sT = sb("sT", [P, 2, CW], at=st)
            bb = sb("bb", [P, 2, CT], at=st)
            bbT = sb("bbT", [CT, 2, P], at=st)
            sel = sb("sel", [CT, CT, P], at=st)
            d2 = sb("d2", [P, 2, CT, T], at=st)

            m_w = [load(act, w_in[:, :], w_inT, "l_win"), load(act, bias[:, 0:2], b_in, "l_bin"),
                   load(act, w_s[:, :], w_sT, "l_ws"), load(act, bias[:, 2:3], b_s, "l_bs"),
                   load(act, w_o[:, :], w_oT, "l_wo")]
            m_bo = load(act, bo[:, :, :], b_o.rearrange("(a b d) -> a b d", a=1, b=1).broadcast_to([P, CT, D]), "l_bo")
            cn_in, cT_in = [], []
            for c in range(NC):
                s = slice(c * CT, (c + 1) * CT)
                if c:
                    x_in.append(load(sp, xr[:, s, :], rows(x)[:, s, :], f"x_in{c}"))
                cn_in.append(load(sp, cn[:, s, :], rows(ctx)[:, s, :], f"cn_in{c}"))
                cT_in.append(load(sp, cT[:, c * CW:(c + 1) * CW], ctxT[:, c * CW:(c + 1) * CW], f"cT_in{c}"))

            m = pool_done(pool.memset(sel[:, :, :], 0.0))
            after(pool, m)
            m_sel = pool_done(pool.affine_select(out=sel[:, :, :], in_=sel[:, :, :], compare_op=ALU.not_equal, fill=1.0,
                                                 base=0, pattern=[[-1, CT], [0, P]], channel_multiplier=1))
            after(act, m_w[1])
            m_nb = act_done(act.mul(bias[:, 3:4], bias[:, 0:1], -1.0))

            X_T, GATE, VAL, SV, OUT, S_T, BB, AB = bank
            hist = {}

            def old(name, c):
                return hist.get((name, c))

            def mark(name, c, m):
                hist[(name, c)] = m
                return m

            def chunk(c):
                b = c % 2
                s = slice(c * CT, (c + 1) * CT)
                m_st = ln_stats(0, c, x_in[c])
                yield
                after(dve, m_st, old("xnT", c - 2), old("xadd", c - 2))
                for t in range(CT):
                    m_xn = normalise(0, c * CT + t, xn[:, b, t, :])
                after(pe, m_xn, m_ident, old("xnT", c - 1))
                for t in range(CT):
                    m = pe_done(pe.transpose(X_T[:, t * P:(t + 1) * P], xn[:, b, t, :], ident[:, :]))
                yield
                after(act, m, old("VALp", c - 2))
                m_xT = mark("xnT", c, act_done(act.copy(xnT[:, b, :], X_T[:, :])))
                after(pe, m_xT, m_w[0], old("keep", c - 1))
                m_g = pe_done(pe.matmul(GATE[:, :], w_in[:, 0:D], xnT[:, b, :], start=True, stop=True))
                after(pe, old("val", c - 1))
                m_v = mark("VALp", c, pe_done(pe.matmul(VAL[:, :], w_in[:, D:2 * D], xnT[:, b, :], start=True, stop=True)))
                after(pool, m_bo, m_xn)
                m = pool_done(pool.tensor_tensor(xr[:, s, :], xr[:, s, :], bo[:, :, :], ALU.add))
                after(pool, m)
                mark("xadd", c, pool_done(pool.tensor_tensor(xr[:, s, :], xr[:, s, :], xn[:, b, :, :], ALU.add)))
                yield
                after(act, m_g, m_nb, m_w[3], old("scan", c - 2), old("b", c - 2))
                act_gate = act_done(act.activation(gate[:, b, :], GATE[:, :], ACT.Sigmoid, bias=bias[:, 0:1]))
                m_keep = mark("keep", c, act_done(act.activation(keep[:, b, :], GATE[:, :], ACT.Sigmoid, bias=bias[:, 3:4], scale=-1.0)))
                after(act, m_v, old("SVp", c - 2))
                m_val = mark("val", c, act_done(act.activation(val[:, b, :], VAL[:, :], ACT.Identity, bias=bias[:, 1:2])))
                after(pe, m_val, m_w[2], old("tanh", c - 1))
                m_s = mark("SVp", c, pe_done(pe.matmul(SV[:, :], w_s[:, :], val[:, b, :], start=True, stop=True)))
                yield
                after(pool, m_keep)
                m_reset = pool_done(pool.memset(keep[:, b, 0:CW:T], 0.0))
                after(act, m_s)
                m_tanh = mark("tanh", c, act_done(act.activation(sv[:, b, :], SV[:, :], ACT.Tanh, bias=bias[:, 2:3])))
                after(pool, m_tanh, act_gate)
                m_b = mark("b", c, pool_done(pool.tensor_tensor(sv[:, b, :], sv[:, b, :], gate[:, b, :], ALU.mult)))
                yield
                after(dve, m_b, m_reset, old("OUTp", c - 2))
                m_h = mark("scan", c, dve_done(dve.tensor_tensor_scan(h[:, b, :], keep[:, b, :], sv[:, b, :], 0.0, ALU.mult, ALU.add)))
                after(pe, m_h, m_w[4], old("x1", c - 1))
                for t in range(CT):
                    m = pe_done(pe.matmul(OUT[:, t * D:(t + 1) * D], h[:, b, t * P:(t + 1) * P], w_o[:, :], start=True, stop=True))
                m_o = mark("OUTp", c, m)
                yield
                after(dve, m_o, old("xadd", c))
                m_x1 = mark("x1", c, dve_done(dve.tensor_tensor(xr[:, s, :], OUT[:, :].rearrange("p (t d) -> p t d", d=D), xr[:, s, :], ALU.add)))
                m_st = ln_stats(1, c, m_x1)
                after(act, cn_in[c])
                for t in range(CT):
                    m_aa = act_done(act.activation(sq[:, :], cn[:, c * CT + t, :], ACT.Square, accum_out=aa[:, c * CT + t:c * CT + t + 1]))
                    after(act, m_aa)
                yield
                after(dve, m_st, old("sTt", c - 2))
                for t in range(CT):
                    m_sn = normalise(1, c * CT + t, sn[:, b, t, :])
                after(pool, m_st, old("bbt", c - 2))
                m = pool_done(pool.tensor_tensor(bb[:, b, :], rstds[:, 1, s], rstds[:, 1, s], ALU.mult))
                after(pool, m)
                m = pool_done(pool.tensor_tensor(bb[:, b, :], bb[:, b, :], mvs[:, 1, s, 1], ALU.mult))
                after(pool, m)
                m_bb = pool_done(pool.tensor_scalar(bb[:, b, :], bb[:, b, :], float(D), None, ALU.mult))
                after(pe, m_sn, m_ident, old("sT", c - 1))
                for t in range(CT):
                    m = pe_done(pe.transpose(S_T[:, t * P:(t + 1) * P], sn[:, b, t, :], ident[:, :]))
                m_t = mark("sTt", c, m)
                after(pe, m_bb, old("bbT", c - 1))
                m_bt = mark("bbt", c, pe_done(pe.transpose(BB[0:CT, 0:P], bb[:, b, :], ident[:, :])))
                yield
                after(act, m_t, old("ABp", c - 2))
                m_sT = mark("sT", c, act_done(act.mul(sT[:, b, :], S_T[:, :], -2.0)))
                after(act, m_bt)
                m_bT = mark("bbT", c, act_done(act.copy(bbT[:, b, :], BB[0:CT, 0:P])))
                after(pe, m_sT, m_bT, m_sel, cT_in[c], old("d2", c - 1))
                for t in range(CT):
                    a = slice(t * P, (t + 1) * P)
                    pe_done(pe.matmul(AB[:, a], cT[:, c * CW + t * P:c * CW + (t + 1) * P], sT[:, b, a], start=True, stop=False))
                    m = pe_done(pe.matmul(AB[:, a], sel[:, t, :], bbT[:, b, :], start=False, stop=True))
                m_ab = mark("ABp", c, m)
                yield
                after(dve, m_ab, m_aa, old("st0", c - 2), old("st1", c - 2))
                ab = AB[:, :].rearrange("p (t q j) -> p t q j", t=CT, q=2)
                for q in range(2):
                    r = slice(q * T, (q + 1) * T)
                    m = dve_done(dve.tensor_tensor(d2[r, b, :, :], ab[r, :, q, :], aa[r, s, None].to_broadcast([T, CT, T]), ALU.add))
                mark("d2", c, m)
                after(pool, m)
                m = pool_done(pool.tensor_scalar(d2[:, b, :, :], d2[:, b, :, :], 0.0, None, ALU.max))
                after(sp, m)
                for q in range(2):
                    seqs = dist[c * 2 * CT + q:(c + 1) * 2 * CT:2, :, :].rearrange("n i j -> i n j")
                    mark(f"st{q}", c, load(sp, seqs, d2[q * T:(q + 1) * T, b, :, :], f"dist{q}_{c}"))

            under_way, started = [], 0
            while under_way or started < NC:
                if started < NC:
                    under_way.append(chunk(started))
                    started += 1
                under_way = [g for g in under_way if next(g, "end") != "end"]

            m_dist = [hist[(f"st{q}", c)] for q in range(2) for c in range(NC)]
            stage1_end = [(t.sem, t.n) for t in (pe_done, dve_done, act_done, pool_done)]

        with ExitStack() as st:
            BR = 8
            NB = T // BR
            MR = 16
            Q = NSEQ
            dd = sb("dd", [Q, T, T], at=st)
            R = sb("R", [Q, T + 1, T + 1], at=st)
            mn = sb("mn", [Q, MR, T], at=st)
            q = sb("q", [Q, 2, BR, T], at=st)
            w = sb("w", [Q, T, T], BF16, at=st)
            left = sb("left", [Q, T, T + 1], BF16, at=st)
            v = sb("v", [Q, T, T + 1], BF16, at=st)
            F = sb("F", [Q, T, T + 1], BF16, at=st)
            dF = sb("dF", [Q, T, T], BF16, at=st)
            junk = sb("junk", [Q, T], BF16, at=st)
            W = sb("W", [Q, T + 1], at=st)
            Wd = sb("Wd", [Q, 2, 2, T], at=st)
            raw = sb("raw", [P, 2, 2 * HID + KC * D], at=st)
            rt_raw = sb("rt_raw", [P, NE + 1], at=st)

            after(sp, *m_dist, *stage1_end)
            blocks = [slice(0, 8), slice(8, 24), slice(24, 44), slice(44, 64)]
            dd_in = [load(sp, dd[:, r, :], dist[:, r, :], f"dd_in{k}") for k, r in enumerate(blocks)]
            for e in (pe, dve, act, pool):
                after(e, *stage1_end, *m_dist)

            pool_done(pool.memset(R[:, 0, :], BIG))
            pool_done(pool.memset(R[:, 1:, 0:1], BIG))
            pool_done(pool.memset(left[:, :, 0:1], 0.0))
            pool_done(pool.memset(v[:, :, 0:1], 0.0))
            pool_done(pool.memset(W[:, 0:1], 0.0))
            m_pads = pool_done(pool.memset(W[:, T:T + 1], float(T - 1)))

            m_dd = []
            for k, r in enumerate(blocks):
                after(act, dd_in[k])
                m_dd.append(act_done(act.activation(dd[:, r, :], dd[:, r, :], ACT.Sqrt)))
            row_dd = [m_dd[next(k for k, r in enumerate(blocks) if r.start <= i < r.stop)] for i in range(T)]

            raw_free = [None, None]
            m_split = []

            def split_weights(e):
                b = e % 2
                after(sp, raw_free[b])
                l1 = load(sp, raw[:, b, 0:2 * HID], w13[:, e, :], f"w13_in{e}")
                l2 = load(sp, raw[:, b, 2 * HID:], w2[:, e, :, :].rearrange("p k d -> p (k d)"), f"w2_in{e}")
                after(act, l1, l2)
                h1 = act_done(act.copy(w13_hi[:, e, :], raw[:, b, 0:2 * HID]))
                raw2 = raw[:, b, 2 * HID:].rearrange("p (k d) -> p k d", k=KC)
                h2 = act_done(act.copy(w2_2[:, e, :, 0, :], raw2))
                after(pool, h1)
                pool_done(pool.tensor_tensor(w13_lo[:, e, :], raw[:, b, 0:2 * HID], w13_hi[:, e, :].bitcast(F32), ALU.subtract))
                after(pool, h2)
                raw_free[b] = pool_done(pool.tensor_tensor(w2_2[:, e, :, 1, :], raw2, w2_2[:, e, :, 0, :].bitcast(F32), ALU.subtract))
                m_split.append(raw_free[b])

            m_scan, m_min, m_left = [None] * T, [None] * T, [None] * T
            m_w, m_F, m_dF, m_v = [None] * NB, [None] * NB, [None] * NB, [None] * T

            def column_of(k):
                r = slice(k * BR, (k + 1) * BR)
                qb = q[:, k % 2, :, :]
                after(pool, m_scan[r.stop - 1], m_w[k - 2] if k >= 2 else m_pads)
                m = pool_done(pool.tensor_tensor(qb, R[:, r, 1:], R[:, r, 0:T], ALU.subtract))
                after(pool, m)
                m = pool_done(pool.tensor_scalar(qb, qb, 0.0, -0.5, ALU.is_ge, ALU.mult))
                after(pool, m, m_iota)
                m_w[k] = pool_done(pool.tensor_tensor(w[:, r, :], qb, iota_f[0:Q, None, 0:T].to_broadcast([Q, BR, T]), ALU.add))

            def choose(i):
                after(dve, m_left[i], m_w[i // BR])
                m_v[i] = dve_done(dve.scalar_tensor_tensor(v[:, i, 1:], left[:, i, 1:], 0.0, w[:, i, :], ALU.is_equal, ALU.mult))

            def spread(k):
                r = slice(k * BR, (k + 1) * BR)
                after(dve, m_v[r.stop - 1])
                flat = [a[:, r, :].rearrange("q i j -> q (i j)") for a in (F, left, v)]
                m_F[k] = dve_done(dve.tensor_tensor_scan(*flat, 0.0, ALU.mult, ALU.add))

            def steps(k):
                r = slice(k * BR, (k + 1) * BR)
                after(pool, m_F[k])
                m_dF[k] = pool_done(pool.tensor_tensor(dF[:, r, :], F[:, r, 1:], F[:, r, 0:T], ALU.subtract))

            LAG = 14
            after(dve, m_pads)
            for i in range(T + LAG):
                if i < T:
                    after(dve, m_scan[i - 1] if i else None, m_left[i - MR] if i >= MR else None)
                    m_min[i] = dve_done(dve.tensor_tensor(mn[:, i % MR, :], R[:, i, 1:], R[:, i, 0:T], ALU.min))
                if 1 <= i <= T:
                    after(dve, m_scan[i - 1], m_min[i - 1])
                    m_left[i - 1] = dve_done(dve.tensor_tensor(left[:, i - 1, 1:], R[:, i, 0:T], mn[:, (i - 1) % MR, :], ALU.is_lt))
                if i < T:
                    after(dve, m_min[i], row_dd[i])
                    m_scan[i] = dve_done(dve.tensor_tensor_scan(R[:, i + 1, 1:], mn[:, i % MR, :], dd[:, i, :],
                                                                BIG if i else 0.0, ALU.min, ALU.add))
                if i >= LAG:
                    choose(i - LAG)
                if i < T and i % BR == BR - 1:
                    column_of(i // BR)
                    split_weights(i // BR)
                if i >= LAG and (i - LAG) % BR == BR - 1:
                    spread((i - LAG) // BR)
                    steps((i - LAG) // BR)

            l = load(sp, rt_raw[:, :], router, "rt_in")
            after(act, l)
            m = act_done(act.copy(rt_hi[:, :], rt_raw[:, :]))
            after(pool, m)
            m_rt = pool_done(pool.tensor_tensor(rt_lo[:, :], rt_raw[:, :], rt_hi[:, :].bitcast(F32), ALU.subtract))

            m = None
            for i in range(T - 1, 0, -1):
                after(dve, m, m_dF[i // BR], m_iota, m_pads)
                m = dve_done(dve.scalar_tensor_tensor(junk[:, :], iota_f[0:Q, 0:T], W[:, i + 1:i + 2], dF[:, i, :], ALU.is_le, ALU.mult,
                                                      accum_out=W[:, i:i + 1]))
            after(dve, m)
            for k in range(2):
                m = dve_done(dve.tensor_copy(Wd[:, k, :, :], W[:, None, k:k + T].to_broadcast([Q, 2, T])))
            WT = bank[0]
            after(pe, m, m_ident)
            for k in range(2):
                m = pe_done(pe.transpose(WT[:, k * Q:(k + 1) * Q], Wd[:, k, :, :].rearrange("q a i -> q (a i)"), ident[0:Q, 0:Q]))
            after(dve, m)
            wt = WT[:, 0:2 * Q].rearrange("p (k n h) -> p k n h", k=2, h=2)
            dve_done(dve.tensor_copy(bounds[0:T, :, :], wt[0:T, :, :, 0]))
            m_bounds = dve_done(dve.tensor_scalar(bounds[T:P, :, :], wt[T:P, :, :, 1], float(T), None, ALU.add))
            stage2_end = [(t.sem, t.n) for t in (pe_done, dve_done, act_done, pool_done)]

        if True:
            st = stack
            mk = sb("mk", [P, 2, CT, P], at=st)
            xT_hi = sb("xT_hi", [P, TOK], F32R, at=st)
            xT_lo = sb("xT_lo", [P, TOK], F32R, at=st)
            pay = sb("pay", [P, NT, ROW], at=st)
            for e in (pe, dve, act, pool, sp):
                after(e, *stage2_end)
            m_id = pool_done(pool.iota(pay[:, :, D + 1:].bitcast(I32), [[P, NT], [1, 1]], base=0, channel_multiplier=1))
            ALIGN, X_T, LOGIT = bank[1], bank[7], bank[0]

            def aligned(c):
                b = c % 2
                s = slice(c * CT, (c + 1) * CT)
                after(dve, m_bounds, m_iota, old("al", c - 2))
                ms = [dve_done(dve.tensor_scalar(mk[:, b, t, :], iota_f[:, :], bounds[:, 1, c * CT + t:c * CT + t + 1], None, ALU.is_le))
                      for t in range(CT)]
                for t in range(CT):
                    n = c * CT + t
                    after(dve, ms[t])
                    m_mk = dve_done(dve.scalar_tensor_tensor(mk[:, b, t, :], iota_f[:, :], bounds[:, 0, n:n + 1], mk[:, b, t, :], ALU.is_ge, ALU.mult))
                after(pe, m_mk, old("x2", c - 1))
                for t in range(CT):
                    m = pe_done(pe.matmul(ALIGN[:, t * D:(t + 1) * D], mk[:, b, t, :], cn[:, c * CT + t, :], start=True, stop=True))
                mark("al", c, m)
                yield
                after(dve, m)
                m_x2 = mark("x2", c, dve_done(dve.tensor_tensor(xr[:, s, :], ALIGN[:, :].rearrange("p (t d) -> p t d", d=D), xr[:, s, :], ALU.add)))
                m_st = ln_stats(2, c, m_x2)
                yield
                after(dve, m_st)
                for t in range(CT):
                    m_n = normalise(2, c * CT + t, pay[:, c * CT + t, 0:D])
                after(pe, m_n, old("xT_lo", c - 1))
                for t in range(CT):
                    m = pe_done(pe.transpose(X_T[:, t * P:(t + 1) * P], pay[:, c * CT + t, 0:D], ident[:, :]))
                yield
                a = slice(c * CW, (c + 1) * CW)
                after(act, m)
                m_hi = mark("xT_hi", c, act_done(act.copy(xT_hi[:, a], X_T[:, :])))
                after(dve, m_hi)
                m_lo = mark("xT_lo", c, dve_done(dve.tensor_tensor(xT_lo[:, a], X_T[:, :], xT_hi[:, a].bitcast(F32), ALU.subtract)))
                after(pe, m_lo, m_hi, m_rt)
                for t in range(CT):
                    n = c * CT + t
                    r = slice(n * P, (n + 1) * P)
                    o = LOGIT[:, n * (NE + 1):(n + 1) * (NE + 1)]
                    pe.matmul(o, xT_hi[:, r], rt_hi[:, :], start=True, stop=False)
                    pe.matmul(o, xT_hi[:, r], rt_lo[:, :], start=False, stop=False)
                    m = pe_done(pe.matmul(o, xT_lo[:, r], rt_hi[:, :], start=False, stop=True))
                mark("logit", c, m)

            under_way, started = [], 0
            while under_way or started < NC:
                if started < NC:
                    under_way.append(aligned(started))
                    started += 1
                under_way = [g for g in under_way if next(g, "end") != "end"]

        with ExitStack() as st:
            def e8(name, dt=F32):
                return sb(name, [P, NT, NE], dt, at=st)
            lg, pr, oh, key, t1 = (e8(n) for n in ("lg", "pr", "oh", "key", "t1"))
            oh_b = e8("oh_b", BF16)
            cnt, incl, base, lt = (sb(n, [P, NE, NT], at=st) for n in ("cnt", "incl", "base", "lt"))
            pm, km, sc, inv, pos = (sb(n, [P, NT], at=st) for n in ("pm", "km", "sc", "inv", "pos"))
            te, ends = (sb(n, [P, NE], at=st) for n in ("te", "ends"))
            ekc = sb("ekc", [1, NS, NE - 1], at=st)
            ekf = sb("ekf", [1, NS], at=st)
            RANK, COUNT = bank[1], bank[6]

            after(dve, old("logit", NC - 1), m_rb)
            lgp = LOGIT[:, 0:NT * (NE + 1)].rearrange("p (n e) -> p n e", e=NE + 1)[:, :, 0:NE]

            def chain(ins):
                m = dve_done(ins)
                after(dve, m)
                return m

            def over_e(a):
                return a[:, :, None].to_broadcast([P, NT, NE])

            chain(dve.tensor_tensor(lg[:, :, :], lgp, rb[:, None, :].to_broadcast([P, NT, NE]), ALU.add))
            m = chain(dve.tensor_scalar(lg[:, :, :], lg[:, :, :], -50.0, 50.0, ALU.max, ALU.min))
            after(act, m)
            m = act_done(act.activation(pr[:, :, :], lg[:, :, :], ACT.Sigmoid))
            after(dve, m)
            chain(dve.tensor_reduce(pm[:, :], pr[:, :, :], AX_X, ALU.max))
            chain(dve.tensor_tensor(oh[:, :, :], pr[:, :, :], over_e(pm), ALU.is_equal))
            chain(dve.tensor_tensor(key[:, :, :], oh[:, :, :], prio[:, None, :].to_broadcast([P, NT, NE]), ALU.mult))
            chain(dve.tensor_reduce(km[:, :], key[:, :, :], AX_X, ALU.max))
            m_oh = chain(dve.tensor_tensor(oh_b[:, :, :], key[:, :, :], over_e(km), ALU.is_equal))
            ohf = oh_b[:, :, :].rearrange("p n e -> p (n e)")
            after(pe, m_oh, m_tri)
            m_rank = pe_done(pe.matmul(RANK[:, 0:NT * NE], tri[:, :], ohf, start=True, stop=True))
            m_cnt = pe_done(pe.matmul(COUNT[:, 0:NT * NE], ones[:, :], ohf, start=True, stop=True))
            chain(dve.tensor_scalar(pm[:, :], pm[:, :], 1e-8, 1.0 - 1e-8, ALU.max, ALU.min))
            chain(dve.tensor_scalar(sc[:, :], pm[:, :], 0.5, 1e-8, ALU.add, ALU.add))
            chain(dve.tensor_scalar(sc[:, :], sc[:, :], 0.5, 2.0, ALU.max, ALU.min))
            chain(dve.reciprocal(inv[:, :], sc[:, :]))
            chain(dve.tensor_tensor(pay[:, :, D], pm[:, :], inv[:, :], ALU.mult))
            m_ws = chain(dve.tensor_scalar(w_sh[:, :], inv[:, :], 0.5, None, ALU.mult))
            after(dve, m_cnt)
            chain(dve.tensor_copy(cnt[:, :, :], COUNT[:, 0:NT * NE].rearrange("p (n e) -> p e n", e=NE)))
            chain(dve.tensor_tensor_scan(incl[:, :, :].rearrange("p e n -> p (e n)"), carry[:, :, :].rearrange("p e n -> p (e n)"),
                                         cnt[:, :, :].rearrange("p e n -> p (e n)"), 0.0, ALU.mult, ALU.add))
            chain(dve.tensor_tensor(lt[:, :, :], i128[:, None, 0:NT].to_broadcast([P, NE, NT]),
                                    incl[:, :, NT - 1:NT].to_broadcast([P, NE, NT]), ALU.is_lt))
            chain(dve.tensor_reduce(te[:, :], lt[:, :, :], AX_X, ALU.add))
            m_ends = chain(dve.tensor_tensor_scan(ends[:, :], onesf[:, 0:NE], te[:, :], 0.0, ALU.mult, ALU.add))
            chain(dve.tensor_tensor(te[:, :], ends[:, :], te[:, :], ALU.subtract))
            chain(dve.tensor_tensor(base[:, :, :], incl[:, :, :], cnt[:, :, :], ALU.subtract))
            chain(dve.scalar_tensor_tensor(base[:, :, :], te[:, :, None].to_broadcast([P, NE, NT]), float(P), base[:, :, :], ALU.mult, ALU.add))
            after(dve, m_rank)
            chain(dve.tensor_tensor(t1[:, :, :], RANK[:, 0:NT * NE].rearrange("p (n e) -> p n e", e=NE),
                                    base[:, :, :].rearrange("p e n -> p n e"), ALU.add))
            chain(dve.tensor_tensor(t1[:, :, :], t1[:, :, :], oh_b[:, :, :], ALU.mult))
            chain(dve.tensor_reduce(pos[:, :], t1[:, :, :], AX_X, ALU.add))
            m_pos = chain(dve.tensor_copy(pos_i[:, :], pos[:, :]))
            chain(dve.tensor_tensor(ekc[:, :, :], ends[0:1, None, 0:NE - 1].to_broadcast([1, NS, NE - 1]),
                                    iota_f[0:1, 0:NS, None].to_broadcast([1, NS, NE - 1]), ALU.is_le))
            chain(dve.tensor_reduce(ekf[:, :], ekc[:, :, :], AX_X, ALU.add))
            chain(dve.tensor_scalar(up_at[:, 0:NS], ekf[:, :], float(2 * HID), None, ALU.mult))
            chain(dve.tensor_scalar(down_at[:, 2:NS + 2], ekf[:, :], float(KC * 2 * D), None, ALU.mult))
            router_end = [(t.sem, t.n) for t in (pe_done, dve_done, act_done)]

        s_put = sem("s_put")
        after(pool, m_pos, m_fill, m_id)
        for n in range(NT):
            pool.indirect_dma_start(routed, bass.IndirectOffsetOnAxis(ap=pos_i[:, n:n + 1], axis=0), pay[:, n, :], None,
                                    bounds_check=NS * P - 1).then_inc(s_put, 16)
        m_put = (s_put, NT * 16)

        for e in (pe, dve, act):
            after(e, *router_end)
        meta = sb("meta", [P, NS, 2])
        slot = sb("slot", [P, 2, 2])
        xs = sb("xs", [P, 2, D])
        yt = sb("yt", [P, NT, D])
        spare = cn[:, :, :].rearrange("p n d -> p (n d)")

        def take(at, *shape):
            n = int(np.prod(shape))
            names = "abc"[:len(shape)]
            return spare[:, at:at + n].rearrange(f"p ({' '.join(names)}) -> p {' '.join(names)}", **dict(zip(names, shape)))

        g = take(0, 2, CW)
        h32 = take(2 * CW, 2, CW)
        y = take(4 * CW, 2, D)
        h_hi = sb("h_hi", [P, 2, KC, CW], F32R)
        h_lo = sb("h_lo", [P, 2, KC, CW], F32R)
        xs_hi = sb("xs_hi", [P, 2, P], F32R)
        xs_lo = sb("xs_lo", [P, 2, P], F32R)

        after(sp, m_put, *router_end)
        m_meta = load(sp, meta[:, :, :], routed.rearrange("(k p) r -> p k r", p=P)[:, :, D:], "meta_in")

        A, U, Y, HT = bank[2:5:2], bank[3:6:2], bank[6:8], bank[0:2]
        free = {}

        def three(o, lhs, rhs):
            (lh, ll), (rh, rl) = lhs, rhs
            return [(o, lh, rh), (o, lh, rl), (o, ll, rh)]

        def products(ps):
            for k, (o, l, r) in enumerate(ps):
                ins = pe.matmul(o, l, r, start=(k == 0), stop=(k == len(ps) - 1))
            return ins

        def down(o, pieces):
            for k, (hh, hl, w) in enumerate(pieces):
                pe.matmul(o, hh, w, start=(k == 0), stop=False, skip_group_check=True)
                ins = pe.matmul(o[:, 0:D], hl, w[:, 0:D], start=False, stop=(k == KC - 1), skip_group_check=True)
            return ins

        def shared(c):
            b = c % 2
            a = slice(c * CW, (c + 1) * CW)
            xT = (xT_hi[:, a], xT_lo[:, a])
            for k in range(KC):
                kw, i = KW[k], (c * KC + k) % 2
                after(pe, m_split[SH], free.get(("U", i)), old("xT_lo", c))
                wa = slice(k * P, k * P + kw)
                wu = slice(HID + k * P, HID + k * P + kw)
                m_a = pe_done(products(three(A[i][0:kw, :], (w13_hi[:, SH, wa], w13_lo[:, SH, wa]), xT)))
                m_u = pe_done(products(three(U[i][0:kw, :], (w13_hi[:, SH, wu], w13_lo[:, SH, wu]), xT)))
                after(act, m_a, free.get(("g", i)))
                m_g = act_done(act.activation(g[0:kw, i, :], A[i][0:kw, :], ACT.Silu))
                after(dve, m_g, m_u, free.get(("h32", i)))
                m = free[("U", i)] = free[("g", i)] = dve_done(dve.tensor_tensor(h32[0:kw, i, :], U[i][0:kw, :], g[0:kw, i, :], ALU.mult))
                after(act, m, free.get(("h", b)) if k == 0 else None)
                m_hi = act_done(act.copy(h_hi[0:kw, b, k, :], h32[0:kw, i, :]))
                after(dve, m_hi)
                m_lo = free[("h32", i)] = dve_done(dve.tensor_tensor(h_lo[0:kw, b, k, :], h32[0:kw, i, :], h_hi[0:kw, b, k, :].bitcast(F32), ALU.subtract))
            return m_lo

        def shared_down(c, m_lo):
            b = c % 2
            after(pe, m_lo, free.get("Y"))
            for t in range(CT):
                r = slice(t * P, (t + 1) * P)
                yb = Y[t // 2][:, (t % 2) * 2 * D:(t % 2 + 1) * 2 * D]
                m = pe_done(down(yb, [(h_hi[0:KW[k], b, k, r], h_lo[0:KW[k], b, k, r], w2_2[0:KW[k], SH, k, :, :].rearrange("p a d -> p (a d)"))
                                      for k in range(KC)]))
            free[("h", b)] = m
            after(dve, m, m_ws)
            ms = []
            for part in range(2):
                for t in range(CT):
                    n = c * CT + t
                    if part:
                        after(dve, ms[t])
                    yb = Y[t // 2][:, (2 * (t % 2) + part) * D:(2 * (t % 2) + part + 1) * D]
                    m = dve_done(dve.scalar_tensor_tensor(xr[:, n, :], yb, w_sh[:, n:n + 1], xr[:, n, :], ALU.mult, ALU.add))
                    ms.append(m)
            free["Y"] = mark("x3", c, m)

        BEFORE = 6
        for c in range(BEFORE):
            m_lo = shared(c)
            if c:
                shared_down(c - 1, m_prev)
            m_prev = m_lo
        shared_down(BEFORE - 1, m_prev)

        all_end = [(t.sem, t.n) for t in (pe_done, dve_done, act_done)]
        for e in (pe, dve, act):
            after(e, *all_end)
        s_x, s_xh, s_xl, s_a, s_u, s_g, s_h, s_t, s_hh, s_hl, s_y, s_ys, s_rn, s_y1 = (sem("tile_" + n) for n in
            ("x", "x_hi", "x_lo", "a", "u", "silu", "h", "hT", "hT_hi", "hT_lo", "y", "y_out", "row_no", "y_part"))
        s_xi = [sem("tile_in0"), sem("tile_in1")]
        s_o = [sem("tile_put0"), sem("tile_put1")]
        X = bank[7]
        ytok = nc.dram_tensor("ytok", [TOK, D], F32, kind="Internal").ap()

        def cols(start, n):
            return slice(start, start + n) if isinstance(start, int) else bass.ds(start, n)

        meta_flat = meta[:, :, :].rearrange("p k r -> p (k r)")

        def x_load(k, i, again):
            if again:
                sp.wait_ge(s_x, k - 1)
            sp.dma_start(xs[:, i, :], routed[cols(k * P, P), 0:D]).then_inc(s_xi[i], 16)

        def x_turn(k, i, pair):
            pe.wait_ge(s_xi[i], (pair + 1) * 16)
            if not isinstance(k, int) or k:
                pe.wait_ge(s_xl, k)
            pe.transpose(X[:, 0:P], xs[:, i, :], ident[:, :]).then_inc(s_x, 1)

        w13_flat_hi = w13_hi[:, :, :].rearrange("p e h -> p (e h)")
        w13_flat_lo = w13_lo[:, :, :].rearrange("p e h -> p (e h)")
        w2_flat = w2_2[:, :, :, :, :].rearrange("p e k a d -> p (e k a d)")

        def x_split(k, i, again):
            act.wait_ge(s_x, k + 1)
            if again:
                act.wait_ge(s_u, k - 1)
            act.copy(xs_hi[:, i, :], X[:, 0:P]).then_inc(s_xh, 1)
            dve.wait_ge(s_xh, k + 1)
            dve.tensor_tensor(xs_lo[:, i, :], X[:, 0:P], xs_hi[:, i, :].bitcast(F32), ALU.subtract).then_inc(s_xl, 1)

        def routed_step(s, j4, pair, do):
            i = j4 % 2
            j = 1 - i
            if "up" in do:
                base = expert_at(up_reg[j4], 2 * HID)
                pe.wait_ge(s_xl, s + 1)
                if "up again" in do:
                    pe.wait_ge(s_h, s - 1)
                xT = (xs_hi[:, i, :], xs_lo[:, i, :])
                for o, off, sg in ((A[i], 0, s_a), (U[i], HID, s_u)):
                    hi = w13_flat_hi[:, bass.ds(base + off, HID)]
                    lo = w13_flat_lo[:, bass.ds(base + off, HID)]
                    products(three(o[:, 0:HID], xT, (hi, lo))).then_inc(sg, 1)
            if j4 == 0:
                pe.load(down_reg, down_at[0:1, cols(s, 4)])
            if j4 == 3:
                pe.load(up_reg, up_at[0:1, cols(s + 1, 4)])
            if "x" in do:
                x_turn(s + 2, i, pair + 1)
            if "turn" in do:
                pe.wait_ge(s_h, s)
                if "turn again" in do:
                    pe.wait_ge(s_hl, s - 2)
                for k in range(KC):
                    ins = pe.transpose(HT[j][0:KW[k], k * P:(k + 1) * P], g[:, j, k * P:k * P + KW[k]], ident[:, :])
                ins.then_inc(s_t, 1)
            if "down" in do:
                base = expert_at(down_reg[j4], KC * 2 * D)
                pe.wait_ge(s_hl, s - 1)
                if "down again" in do:
                    pe.wait_ge(s_ys, s - 2)
                down(Y[0][:, 0:2 * D], [(h_hi[0:KW[k], i, k, 0:P], h_lo[0:KW[k], i, k, 0:P], w2_flat[0:KW[k], bass.ds(base + k * 2 * D, 2 * D)])
                                        for k in range(KC)]).then_inc(s_y, 1)
            if "up" in do:
                act.wait_ge(s_a, s + 1)
                if "up again" in do:
                    act.wait_ge(s_t, s - 1)
                act.activation(g[:, i, 0:HID], A[i][:, 0:HID], ACT.Silu).then_inc(s_g, 1)
                dve.wait_ge(s_u, s + 1)
                dve.wait_ge(s_g, s + 1)
                dve.tensor_tensor(g[:, i, 0:HID], U[i][:, 0:HID], g[:, i, 0:HID], ALU.mult).then_inc(s_h, 1)
            if "x" in do:
                x_split(s + 2, i, True)
            if "turn" in do:
                act.wait_ge(s_t, s)
                if "turn again" in do:
                    act.wait_ge(s_y, s - 2)
                act.copy(h_hi[:, j, 0:2, 0:P], HT[j][:, 0:2 * P].rearrange("p (k t) -> p k t", k=2)).then_inc(s_hh, 1)
                act.copy(h_hi[0:KW[2], j, 2, 0:P], HT[j][0:KW[2], 2 * P:3 * P]).then_inc(s_hh, 1)
                dve.wait_ge(s_hh, s * 2)
                dve.tensor_tensor(h_lo[:, j, 0:2, 0:P], HT[j][:, 0:2 * P].rearrange("p (k t) -> p k t", k=2),
                                  h_hi[:, j, 0:2, 0:P].bitcast(F32), ALU.subtract)
                dve.tensor_tensor(h_lo[0:KW[2], j, 2, 0:P], HT[j][0:KW[2], 2 * P:3 * P],
                                  h_hi[0:KW[2], j, 2, 0:P].bitcast(F32), ALU.subtract).then_inc(s_hl, 1)
            if "down" in do:
                if "put again" in do:
                    dve.wait_ge(s_o[i], (pair - 1) * 16)
                dve.tensor_copy(slot[:, i, :], meta_flat[:, cols((s - 2) * 2, 2)]).then_inc(s_rn, 1)
                dve.wait_ge(s_rn, s - 1)
                dve.wait_ge(s_y, s - 1)
                weight = slot[:, i, 0:1]
                dve.tensor_scalar(y[:, i, :], Y[0][:, 0:D], weight, None, ALU.mult).then_inc(s_y1, 1)
                dve.wait_ge(s_y1, s - 1)
                dve.scalar_tensor_tensor(y[:, i, :], Y[0][:, D:2 * D], weight, y[:, i, :], ALU.mult, ALU.add).then_inc(s_ys, 1)
                if isinstance(s, int):
                    pool.wait_ge(s_ys, s - 1)
                else:
                    pool.wait_ge(s_ys, y_due)
                    pool.reg_add(y_due, y_due, 1)
                pool.indirect_dma_start(ytok, bass.IndirectOffsetOnAxis(ap=slot[:, i, 1:2].bitcast(U32), axis=0),
                                        y[:, i, :], None, bounds_check=TOK - 1, oob_is_err=False).then_inc(s_o[i], 16)
            if "load" in do:
                x_load(s + 4, i, True)

        after(dve, m_meta)
        after(pool, m_meta)
        for k in range(4):
            x_load(k, k % 2, k >= 2)
            if k < 2:
                x_turn(k, k, 0)
                x_split(k, k, False)

        y_due = pool.alloc_register("y_due")
        up_reg = [pe.alloc_register(f"up_expert{k}") for k in range(4)]
        down_reg = [pe.alloc_register(f"down_expert{k}") for k in range(4)]

        def expert_at(reg, step):
            return pe.snap(reg, min_val=0, max_val=(NE - 1) * step)

        def parts(s):
            has = {"up": s < NS, "up again": 2 <= s, "turn": 1 <= s <= NS, "turn again": 3 <= s, "down": 2 <= s,
                   "down again": 3 <= s, "put again": 4 <= s, "x": s + 2 < NS, "load": s + 4 < NS}
            return {k for k, yes in has.items() if yes}

        pe.load(up_reg, up_at[0:1, 0:4])
        for s in range(4):
            routed_step(s, s, s // 2, parts(s))
        FULL = (NS - 4) // 4 - 1
        pool.reg_mov(y_due, 3)
        with nc.Fori(1, 1 + FULL) as blk:
            for j4 in range(4):
                routed_step(blk * 4 + j4, j4, blk * 2 + j4 // 2, parts(4))
        for s in range((1 + FULL) * 4, NS + 2):
            routed_step(s, s % 4, s // 2, parts(s))

        m_y = [(s_o[0], 16 * (NS // 2)), (s_o[1], 16 * (NS // 2))]
        after(sp, *m_y)
        yt_in = [load(sp, yt[:, c * CT:(c + 1) * CT, :], ytok.rearrange("(n p) d -> p n d", p=P)[:, c * CT:(c + 1) * CT, :], f"y_in{c}")
                 for c in range(NC)]

        def finish(c):
            s = slice(c * CT, (c + 1) * CT)
            after(dve, yt_in[c], old("x3", c))
            m = dve_done(dve.tensor_tensor(xr[:, s, :], xr[:, s, :], yt[:, s, :], ALU.add))
            after(sp, m)
            mark("out", c, load(sp, rows(out)[:, s, :], xr[:, s, :], f"out{c}"))

        for c in range(BEFORE, NC):
            m_lo = shared(c)
            if c == BEFORE:
                for q in range(BEFORE):
                    finish(q)
            shared_down(c, m_lo)
            finish(c)
        after(sp, *(old("out", c) for c in range(NC)))


_OUTS = [((64, 64, 128), "float32")]


def kernel(**inputs):
    import numpy as _np
    import concourse.bacc as _bacc
    from concourse import mybir as _mybir
    from concourse.bass_utils import run_bass_kernel_spmd as _run

    g = {k.replace("L0_", ""): _np.asarray(v) for k, v in inputs.items()}
    w1 = _np.concatenate([g["ffn_ew1"], g["ffn_sw1"][None]])
    w3 = _np.concatenate([g["ffn_ew3"], g["ffn_sw3"][None]])
    w2 = _np.concatenate([g["ffn_ew2"], g["ffn_sw2"][None]])
    w13 = _np.concatenate([w1, w3], axis=1).transpose(2, 0, 1)
    w2p = _np.zeros((NE + 1, D, KC * P), w2.dtype)
    w2p[:, :, :HID] = w2
    w2p = w2p.reshape(NE + 1, D, KC, P).transpose(3, 0, 2, 1)
    rt = _np.zeros((D, NE + 1), g["ffn_router_w"].dtype)
    rt[:, :NE] = g["ffn_router_w"].T
    args_np = {
        "x": g["x"], "ctx": g["ctx_1024"], "ctxT": g["ctx_1024"].reshape(TOK, D).T,
        "w_inT": g["attn_W_in"].T, "b_in": g["attn_b_in"].reshape(2, D).T, "w_sT": g["attn_W_s"].T, "b_s": g["attn_b_s"].reshape(1, D).T,
        "w_oT": g["attn_W_o"].T, "b_o": g["attn_b_o"], "router": rt, "r_bias": g["ffn_routing_bias"],
        "w13": w13, "w2": w2p,
    }
    nc = _bacc.Bacc("TRN2", target_bir_lowering=False, num_devices=1)
    arrays, args = {}, []
    for name, a in args_np.items():
        a = _np.ascontiguousarray(a)
        arrays[f"in_{name}"] = a
        args.append(nc.dram_tensor(f"in_{name}", a.shape, _mybir.dt.from_np(a.dtype), kind="ExternalInput").ap())
    args.append(nc.dram_tensor("out_0", (64, 64, 128), _mybir.dt.float32, kind="ExternalOutput").ap())
    program(nc, *args)
    r = _run(nc, [arrays], core_ids=[0])
    return r.results[0]["out_0"]
```

```python
from contextlib import ExitStack

import numpy as np
import concourse.bass as bass
from concourse import mybir

F32 = mybir.dt.float32
F32R = mybir.dt.float32r
BF16 = mybir.dt.bfloat16
I32 = mybir.dt.int32
U32 = mybir.dt.uint32
ALU = mybir.AluOpType
ACT = mybir.ActivationFunctionType
AX_X = mybir.AxisListType.X

P = 128
NSEQ, T, D = 64, 64, 128
TOK = NSEQ * T
NT = TOK // P
CT = 4
NC = NT // CT
CW = CT * P
NE = 7
SH = NE
HID = 352
KC = 3
KW = [128, 128, HID - 256]
NS = (TOK - NE) // P + NE
NB4 = (NS + 2) // 4
ROW = D + 2
EPS = 1e-5
BIG = 1e30


class Track:

    def __init__(self, sem):
        self.sem, self.n = sem, 0

    def __call__(self, ins, by=1):
        self.n += by
        ins.then_inc(self.sem, by)
        return (self.sem, self.n)


def after(eng, *marks):
    for m in marks:
        if m is not None:
            eng.wait_ge(m[0], m[1])


def program(nc, x, ctx, ctxT, w_inT, b_in, w_sT, b_s, w_oT, b_o, router, r_bias, w13, w2, out):
    pe, dve, act, pool, sp = nc.tensor, nc.vector, nc.scalar, nc.gpsimd, nc.sync
    stack = ExitStack()
    with stack:
        def sem(name):
            return stack.enter_context(nc.semaphore(name))

        def sb(name, shape, dt=F32, at=stack):
            return at.enter_context(nc.sbuf_tensor(name, shape, dt))

        pe_done, dve_done, act_done, pool_done = (Track(sem(n)) for n in ("pe_done", "dve_done", "act_done", "pool_done"))
        bank = [stack.enter_context(nc.psum_tensor(f"bank{i}", [P, 512], F32)) for i in range(8)]

        def load(eng, dst, src, name):
            s = sem(name)
            eng.dma_start(dst, src).then_inc(s, 16)
            return (s, 16)

        def rows(ap):
            return ap.rearrange("b t d -> (b t) d").rearrange("(n p) d -> p n d", p=P)

        dist = nc.dram_tensor("dist", [NSEQ, T, T], F32, kind="Internal").ap()
        x3 = nc.dram_tensor("x3", [TOK, D], F32, kind="Internal").ap()
        routed = nc.dram_tensor("routed", [NS * P, ROW], F32, kind="Internal").ap()

        xr = sb("xr", [P, NT, D])
        w13_hi = sb("w13_hi", [P, NE + 1, 2 * HID], F32R)
        w13_lo = sb("w13_lo", [P, NE + 1, 2 * HID], F32R)
        w2_2 = sb("w2_2", [P, NE + 1, KC, 2, D], F32R)
        rt_2 = sb("rt_2", [P, 2, NE + 1], F32R)
        ident = sb("ident", [P, P])
        iota_i = sb("iota_i", [P, P], I32)
        iota_f = sb("iota_f", [P, P])
        half = sb("half", [P, NT])
        minus = sb("minus", [P, NT])
        scratch = sb("scratch", [1, 1])
        BNR = 4
        bn = sb("bn", [P, BNR, CT, 6])
        mvs = sb("mvs", [P, 3, NT, 2])
        ve = sb("ve", [P, 3, NT])
        rstds = sb("rstds", [P, 3, NT])

        x_in = [load(sp, xr[:, c * CT:(c + 1) * CT, :], rows(x)[:, c * CT:(c + 1) * CT, :], f"x_in{c}") for c in range(1)]

        cn = sb("cn", [P, NT, D])
        bounds = sb("bounds", [P, 2, NT])

        def fetch_table(func):
            act_done(act.activation(scratch[:, :], ident[0:1, 0:1], func))
            after(act, (act_done.sem, act_done.n))

        m = pool_done(pool.memset(ident[:, :], 0.0))
        after(pool, m)
        m_ident = pool_done(pool.affine_select(out=ident[:, :], in_=ident[:, :], compare_op=ALU.not_equal, fill=1.0,
                                               base=0, pattern=[[-1, P]], channel_multiplier=1))
        m = pool_done(pool.iota(iota_i[:, :], [[1, P]], base=0, channel_multiplier=0))
        after(pool, m)
        m_iota = pool_done(pool.tensor_copy(iota_f[:, :], iota_i[:, :]))
        m_half = pool_done(pool.memset(half[:, :], -0.5))
        m_minus = pool_done(pool.memset(minus[:, :], -1.0))

        rb = sb("rb", [P, NE])
        prio = sb("prio", [P, NE])
        prio_i = sb("prio_i", [P, NE], I32)
        tri = sb("tri", [P, P], BF16)
        ones = sb("ones", [P, P], BF16)
        onesf = sb("onesf", [P, NE])
        i128_i = sb("i128_i", [P, NT], I32)
        i128 = sb("i128", [P, NT])
        carry = sb("carry", [P, NE, NT])
        w_sh = sb("w_sh", [P, NT])
        pos_i = sb("pos_i", [P, NT], I32)
        up_at = sb("up_at", [1, NB4 * 4 + 4], I32)
        down_at = sb("down_at", [1, NB4 * 4], I32)
        fill = sb("fill", [P, ROW])

        bn_read = []

        def ln_stats(k, c, src_ready):
            g = len(bn_read) % BNR
            after(dve, src_ready, bn_read[-BNR] if len(bn_read) >= BNR else None)
            marks = [dve_done(dve.bn_stats(bn[:, g, t, :], xr[:, c * CT + t, :])) for t in range(CT)]
            for t in range(CT):
                after(dve, marks[t])
                m = dve_done(dve.bn_aggr(mvs[:, k, c * CT + t, :], bn[:, g, t, :]))
            bn_read.append(m)
            s = slice(c * CT, (c + 1) * CT)
            after(pool, m, m_half)
            m2 = pool_done(pool.tensor_scalar(ve[:, k, s], mvs[:, k, s, 1], EPS, None, ALU.add))
            after(pool, m2)
            return pool_done(pool.tensor_tensor(rstds[:, k, s], ve[:, k, s], half[:, s], ALU.pow))

        def normalise(k, n, dst):
            return dve_done(dve.tensor_scalar(dst, xr[:, n, :], mvs[:, k, n, 0:1], rstds[:, k, n:n + 1], ALU.subtract, ALU.mult))

        with ExitStack() as st:
            w_in = sb("w_in", [P, 2 * D], at=st)
            w_s = sb("w_s", [P, D], at=st)
            w_o = sb("w_o", [P, D], at=st)
            bias = sb("bias", [P, 4], at=st)
            bo = sb("bo", [2, D], at=st)
            bo_hi = sb("bo_hi", [2, D], F32R, at=st)
            bo_lo = sb("bo_lo", [2, D], at=st)
            bo_2 = sb("bo_2", [2, D], F32R, at=st)
            one = sb("one", [2, P], at=st)
            one_r = sb("one_r", [2, P], F32R, at=st)
            cT = sb("cT", [P, TOK], at=st)
            aa = sb("aa", [P, NT], at=st)
            sq = sb("sq", [P, D], at=st)
            xn = sb("xn", [P, 2, CT, D], at=st)
            xnT = sb("xnT", [P, 2, CW], at=st)
            gate = sb("gate", [P, 2, CW], at=st)
            keep = sb("keep", [P, 2, CW], at=st)
            val = sb("val", [P, 2, CW], at=st)
            sv = sb("sv", [P, 2, CW], at=st)
            h = sb("h", [P, 2, CW], at=st)
            sn = sb("sn", [P, 2, CT, D], at=st)
            sT = sb("sT", [P, 2, CW], at=st)
            bb = sb("bb", [P, 2, CT], at=st)
            bbT = sb("bbT", [CT, 2, P], at=st)
            sel = sb("sel", [CT, CT, P], at=st)
            d2 = sb("d2", [P, 2, CT, T], at=st)

            m_w = [load(act, w_in[:, :], w_inT, "l_win"), load(act, bias[:, 0:2], b_in, "l_bin"),
                   load(act, w_s[:, :], w_sT, "l_ws"), load(act, bias[:, 2:3], b_s, "l_bs"),
                   load(act, w_o[:, :], w_oT, "l_wo")]
            m_bo = load(act, bo[:, :], b_o.rearrange("(a d) -> a d", a=1).broadcast_to([2, D]), "l_bo")
            cn_in, cT_in = [], []
            for c in range(NC):
                s = slice(c * CT, (c + 1) * CT)
                if c:
                    x_in.append(load(sp, xr[:, s, :], rows(x)[:, s, :], f"x_in{c}"))
                cn_in.append(load(sp, cn[:, s, :], rows(ctx)[:, s, :], f"cn_in{c}"))
                cT_in.append(load(sp, cT[:, c * CW:(c + 1) * CW], ctxT[:, c * CW:(c + 1) * CW], f"cT_in{c}"))

            m = pool_done(pool.memset(sel[:, :, :], 0.0))
            after(pool, m)
            m_sel = pool_done(pool.affine_select(out=sel[:, :, :], in_=sel[:, :, :], compare_op=ALU.not_equal, fill=1.0,
                                                 base=0, pattern=[[-1, CT], [0, P]], channel_multiplier=1))
            after(act, m_ident)
            fetch_table(ACT.Sigmoid)
            after(act, m_w[1])
            m_nb = act_done(act.mul(bias[:, 3:4], bias[:, 0:1], -1.0))

            X_T, GATE, VAL, SV, OUT, S_T, BB, AB = bank
            hist = {}

            def old(name, c):
                return hist.get((name, c))

            def mark(name, c, m):
                hist[(name, c)] = m
                return m

            def chunk(c):
                b = c % 2
                s = slice(c * CT, (c + 1) * CT)
                m_st = ln_stats(0, c, x_in[c])
                yield
                after(dve, m_st, old("xnT", c - 2), old("xadd", c - 2))
                for t in range(CT):
                    m_xn = normalise(0, c * CT + t, xn[:, b, t, :])
                after(pe, m_xn, m_ident, old("xnT", c - 1))
                for t in range(CT):
                    m = pe_done(pe.transpose(X_T[:, t * P:(t + 1) * P], xn[:, b, t, :], ident[:, :]))
                yield
                after(act, m, old("VALp", c - 2))
                m_xT = mark("xnT", c, act_done(act.copy(xnT[:, b, :], X_T[:, :])))
                after(pe, m_xT, m_w[0], old("keep", c - 1))
                m_g = pe_done(pe.matmul(GATE[:, :], w_in[:, 0:D], xnT[:, b, :], start=True, stop=True))
                after(pe, old("val", c - 1))
                m_v = mark("VALp", c, pe_done(pe.matmul(VAL[:, :], w_in[:, D:2 * D], xnT[:, b, :], start=True, stop=True)))
                after(pool, m_xn)
                mark("xadd", c, pool_done(pool.tensor_tensor(xr[:, s, :], xr[:, s, :], xn[:, b, :, :], ALU.add)))
                yield
                after(act, m_g, m_nb, m_w[3], old("scan", c - 2), old("b", c - 2))
                act_gate = act_done(act.activation(gate[:, b, :], GATE[:, :], ACT.Sigmoid, bias=bias[:, 0:1]))
                m_keep = mark("keep", c, act_done(act.activation(keep[:, b, :], GATE[:, :], ACT.Sigmoid, bias=bias[:, 3:4], scale=-1.0)))
                after(act, m_v, old("SVp", c - 2))
                m_val = mark("val", c, act_done(act.activation(val[:, b, :], VAL[:, :], ACT.Identity, bias=bias[:, 1:2])))
                after(pe, m_val, m_w[2], old("tanh", c - 1))
                m_s = mark("SVp", c, pe_done(pe.matmul(SV[:, :], w_s[:, :], val[:, b, :], start=True, stop=True)))
                yield
                after(pool, m_keep)
                m_reset = pool_done(pool.memset(keep[:, b, 0:CW:T], 0.0))
                after(act, m_s)
                m_tanh = mark("tanh", c, act_done(act.activation(sv[:, b, :], SV[:, :], ACT.Tanh, bias=bias[:, 2:3])))
                after(pool, m_tanh, act_gate)
                m_b = mark("b", c, pool_done(pool.tensor_tensor(sv[:, b, :], sv[:, b, :], gate[:, b, :], ALU.mult)))
                yield
                after(dve, m_b, m_reset, old("OUTp", c - 2))
                m_h = mark("scan", c, dve_done(dve.tensor_tensor_scan(h[:, b, :], keep[:, b, :], sv[:, b, :], 0.0, ALU.mult, ALU.add)))
                after(pe, m_bo_lo, old("x1", c - 1))
                pe_done(pe.matmul(OUT[:, :], one_r[:, :], bo_2[:, None, :].to_broadcast([2, CT, D]), start=True, stop=False, skip_group_check=True))
                after(pe, m_h, m_w[4])
                for t in range(CT):
                    m = pe_done(pe.matmul(OUT[:, t * D:(t + 1) * D], h[:, b, t * P:(t + 1) * P], w_o[:, :], start=False, stop=True, skip_group_check=True))
                m_o = mark("OUTp", c, m)
                yield
                after(dve, m_o, old("xadd", c))
                m_x1 = mark("x1", c, dve_done(dve.tensor_tensor(xr[:, s, :], OUT[:, :].rearrange("p (t d) -> p t d", d=D), xr[:, s, :], ALU.add)))
                m_st = ln_stats(1, c, m_x1)
                after(act, cn_in[c])
                for t in range(CT):
                    m_aa = act_done(act.activation(sq[:, :], cn[:, c * CT + t, :], ACT.Square, accum_out=aa[:, c * CT + t:c * CT + t + 1]))
                    after(act, m_aa)
                yield
                after(dve, m_st, old("sTt", c - 2))
                for t in range(CT):
                    m_sn = normalise(1, c * CT + t, sn[:, b, t, :])
                after(pool, m_st, old("bbt", c - 2))
                m = pool_done(pool.tensor_tensor(bb[:, b, :], rstds[:, 1, s], rstds[:, 1, s], ALU.mult))
                after(pool, m)
                m = pool_done(pool.tensor_tensor(bb[:, b, :], bb[:, b, :], mvs[:, 1, s, 1], ALU.mult))
                after(pool, m)
                m_bb = pool_done(pool.tensor_scalar(bb[:, b, :], bb[:, b, :], float(D), None, ALU.mult))
                after(pe, m_sn, m_ident, old("sT", c - 1))
                for t in range(CT):
                    m = pe_done(pe.transpose(S_T[:, t * P:(t + 1) * P], sn[:, b, t, :], ident[:, :]))
                m_t = mark("sTt", c, m)
                after(pe, m_bb, old("bbT", c - 1))
                m_bt = mark("bbt", c, pe_done(pe.transpose(BB[0:CT, 0:P], bb[:, b, :], ident[:, :])))
                yield
                after(act, m_t, old("ABp", c - 2))
                m_sT = mark("sT", c, act_done(act.mul(sT[:, b, :], S_T[:, :], -2.0)))
                after(act, m_bt)
                m_bT = mark("bbT", c, act_done(act.copy(bbT[:, b, :], BB[0:CT, 0:P])))
                after(pe, m_sT, m_bT, m_sel, cT_in[c], old("d2", c - 1))
                for t in range(CT):
                    a = slice(t * P, (t + 1) * P)
                    pe_done(pe.matmul(AB[:, a], cT[:, c * CW + t * P:c * CW + (t + 1) * P], sT[:, b, a], start=True, stop=False))
                    m = pe_done(pe.matmul(AB[:, a], sel[:, t, :], bbT[:, b, :], start=False, stop=True))
                m_ab = mark("ABp", c, m)
                yield
                after(dve, m_ab, m_aa, old("st0", c - 2), old("st1", c - 2))
                for q in range(2):
                    r = slice(q * T, (q + 1) * T)
                    for t in range(CT):
                        m = dve_done(dve.tensor_scalar(d2[r, b, t, :], AB[r, t * P + q * T:t * P + (q + 1) * T],
                                                       aa[r, c * CT + t:c * CT + t + 1], 0.0, ALU.add, ALU.max))
                    after(sp, m)
                    seqs = dist[c * 2 * CT + q:(c + 1) * 2 * CT:2, :, :].rearrange("n i j -> i n j")
                    mark(f"st{q}", c, load(sp, seqs, d2[r, b, :, :], f"dist{q}_{c}"))
                mark("d2", c, m)

            def split_bias():
                m = pool_done(pool.memset(one[:, :], 1.0))
                after(act, m, m_bo)
                act_done(act.copy(one_r[:, :], one[:, :]))
                m = act_done(act.copy(bo_hi[:, :], bo[:, :]))
                after(dve, m, m_ident)
                m = dve_done(dve.tensor_tensor(bo_lo[:, :], bo[:, :], bo_hi[:, :].bitcast(F32), ALU.subtract))
                after(dve, m)
                m = dve_done(dve.tensor_scalar(bo_lo[:, :], bo_lo[:, :], ident[0:2, 1:2], None, ALU.mult))
                after(dve, m)
                return dve_done(dve.scalar_tensor_tensor(bo_2[:, :], bo_hi[:, :].bitcast(F32), ident[0:2, 0:1], bo_lo[:, :], ALU.mult, ALU.add))

            under_way, started = [], 0
            while under_way or started < NC:
                if started < NC:
                    under_way.append(chunk(started))
                    started += 1
                if started == 3:
                    m_bo_lo = split_bias()
                under_way = [g for g in under_way if next(g, "end") != "end"]

            m_dist = [hist[(f"st{q}", c)] for q in range(2) for c in range(NC)]
            stage1_end = [(t.sem, t.n) for t in (pe_done, dve_done, act_done, pool_done)]

        m_rb = load(act, rb[:, :], r_bias.rearrange("(a e) -> a e", a=1).broadcast_to([P, NE]), "l_rb")
        m1 = pool_done(pool.iota(prio_i[:, :], [[-1, NE]], base=NE, channel_multiplier=0))
        m2 = pool_done(pool.iota(i128_i[:, :], [[P, NT]], base=0, channel_multiplier=0))
        after(pool, m1)
        pool_done(pool.tensor_copy(prio[:, :], prio_i[:, :]))
        after(pool, m2)
        pool_done(pool.tensor_copy(i128[:, :], i128_i[:, :]))
        pool_done(pool.memset(ones[:, :], 1.0))
        pool_done(pool.memset(onesf[:, :], 1.0))
        pool_done(pool.memset(up_at[:, :], 0))
        pool_done(pool.memset(down_at[:, :], 0))
        m1 = pool_done(pool.memset(tri[:, :], 1.0))
        m2 = pool_done(pool.memset(carry[:, :, :], 1.0))
        m3 = pool_done(pool.memset(fill[:, :], 0.0))
        after(pool, m1)
        pool_done(pool.affine_select(out=tri[:, :], in_=tri[:, :], compare_op=ALU.is_gt, fill=0.0,
                                     base=0, pattern=[[1, P]], channel_multiplier=-1))
        after(pool, m2)
        pool_done(pool.memset(carry[:, :, 0:1], 0.0))
        after(pool, m3)
        m_tri = pool_done(pool.memset(fill[:, ROW - 1:ROW].bitcast(I32), 1 << 20))

        loan = sb("loan", [P, NT, D])
        SLOTS = 3
        raw = loan[:, :, :].rearrange("p n d -> p (n d)")[:, 0:SLOTS * (2 * HID + KC * D)].rearrange("p (s w) -> p s w", s=SLOTS)

        with ExitStack() as st:
            BR = 8
            NB = T // BR
            MR = 16
            Q = NSEQ
            dd = sb("dd", [Q, T, T], at=st)
            four = sb("four", [Q, T], at=st)
            four_less_1 = sb("four_less_1", [Q, T], at=st)
            R = sb("R", [Q, T + 1, T + 1], at=st)
            mn = sb("mn", [Q, MR, T], at=st)
            q = sb("q", [Q, 2, BR, T], at=st)
            w = sb("w", [Q, T, T], BF16, at=st)
            left = sb("left", [Q, T, T + 1], BF16, at=st)
            v = sb("v", [Q, T, T + 1], BF16, at=st)
            F = sb("F", [Q, T, T + 1], BF16, at=st)
            dF = sb("dF", [Q, T, T], BF16, at=st)
            junk = sb("junk", [Q, T], BF16, at=st)
            W = sb("W", [Q, T + 1], at=st)
            Wd = sb("Wd", [Q, 2, 2, T], at=st)
            rt_raw = sb("rt_raw", [P, NE + 1], at=st)

            fetch_table(ACT.Sqrt)
            after(sp, *m_dist, *stage1_end)
            blocks = [slice(0, 4), slice(4, 16), slice(16, 40), slice(40, 64)]
            dd_in = [load(sp, dd[:, r, :], dist[:, r, :], f"dd_in{k}") for k, r in enumerate(blocks)]
            for e in (pe, dve, act, pool):
                after(e, *stage1_end, *m_dist)

            pool_done(pool.memset(R[:, 0, :], BIG))
            pool_done(pool.memset(R[:, 1:, 0:1], BIG))
            pool_done(pool.memset(left[:, :, 0:1], 0.0))
            pool_done(pool.memset(v[:, :, 0:1], 0.0))
            pool_done(pool.memset(W[:, 0:1], 0.0))
            after(pool, m_iota)
            pool_done(pool.tensor_scalar(four[:, :], iota_f[0:Q, 0:T], 4.0, None, ALU.mult))
            pool_done(pool.tensor_scalar(four_less_1[:, :], iota_f[0:Q, 0:T], 4.0, -1.0, ALU.mult, ALU.add))
            m_pads = pool_done(pool.memset(W[:, T:T + 1], 4.0 * (T - 1)))

            m_dd = []
            for k, r in enumerate(blocks):
                after(act, dd_in[k])
                m_dd.append(act_done(act.activation(dd[:, r, :], dd[:, r, :], ACT.Sqrt)))
            after(act, m_tri)
            m_fill = load(act, routed.rearrange("(k p) r -> p k r", p=P), fill[:, None, :].to_broadcast([P, NS, ROW]), "fill_out")
            row_dd = [m_dd[next(k for k, r in enumerate(blocks) if r.start <= i < r.stop)] for i in range(T)]

            raw_in, m_high, m_split = {}, {}, {}

            def fetch(e):
                slot_e = raw[:, e % SLOTS, :]
                after(sp, m_split.get(e + SLOTS))
                raw_in[e] = (load(sp, slot_e[:, 0:2 * HID], w13[:, e, :], f"w13_in{e}"),
                             load(sp, slot_e[:, 2 * HID:], w2[:, e, :, :].rearrange("p k d -> p (k d)"), f"w2_in{e}"))

            def parts_of(e):
                slot_e = raw[:, e % SLOTS, :]
                return ((slot_e[:, 0:2 * HID], w13_hi[:, e, :], w13_lo[:, e, :]),
                        (slot_e[:, 2 * HID:].rearrange("p (k d) -> p k d", k=KC), w2_2[:, e, :, 0, :], w2_2[:, e, :, 1, :]))

            def high_parts(e):
                after(act, *raw_in[e])
                m_high[e] = [act_done(act.copy(hi, a)) for a, hi, lo in parts_of(e)]

            def low_parts(e):
                for k, (a, hi, lo) in enumerate(parts_of(e)):
                    after(pool, m_high[e][k])
                    m_split[e] = pool_done(pool.tensor_tensor(lo, a, hi.bitcast(F32), ALU.subtract))

            for e in range(NE, NE - SLOTS, -1):
                fetch(e)

            m_scan, m_min, m_left = [None] * T, [None] * T, [None] * T
            m_sign = [None] * NB
            m_w, m_F, m_dF, m_v = [None] * NB, [None] * NB, [None] * NB, [None] * T

            def column_of(k):
                r = slice(k * BR, (k + 1) * BR)
                qb = q[:, k % 2, :, :]
                after(pool, m_scan[r.stop - 1], m_w[k - 2] if k >= 2 else m_pads)
                m = pool_done(pool.tensor_tensor(qb, R[:, r, 1:], R[:, r, 0:T], ALU.subtract))
                after(act, m)
                m_sign[k] = act_done(act.activation(qb, qb, ACT.Sign))

            def column_end(k):
                r = slice(k * BR, (k + 1) * BR)
                after(pool, m_sign[k], m_pads)
                m_w[k] = pool_done(pool.tensor_tensor(w[:, r, :], four_less_1[0:Q, None, :].to_broadcast([Q, BR, T]), q[:, k % 2, :, :], ALU.subtract))

            def choose(i):
                after(dve, m_left[i], m_w[i // BR])
                m_v[i] = dve_done(dve.scalar_tensor_tensor(v[:, i, 1:], left[:, i, 1:], 0.0, w[:, i, :], ALU.is_equal, ALU.mult))

            def spread(k):
                r = slice(k * BR, (k + 1) * BR)
                after(dve, m_v[r.stop - 1])
                flat = [a[:, r, :].rearrange("q i j -> q (i j)") for a in (F, left, v)]
                m_F[k] = dve_done(dve.tensor_tensor_scan(*flat, 0.0, ALU.mult, ALU.add))

            def steps(k):
                r = slice(k * BR, (k + 1) * BR)
                after(pool, m_F[k])
                m_dF[k] = pool_done(pool.tensor_tensor(dF[:, r, :], F[:, r, 1:], F[:, r, 0:T], ALU.subtract))

            LAG = 16
            after(dve, m_pads)
            for i in range(T + LAG):
                if i < T:
                    after(dve, m_scan[i - 1] if i else None, m_left[i - MR] if i >= MR else None)
                    m_min[i] = dve_done(dve.tensor_tensor(mn[:, i % MR, :], R[:, i, 1:], R[:, i, 0:T], ALU.min))
                if 1 <= i <= T:
                    after(dve, m_scan[i - 1], m_min[i - 1])
                    m_left[i - 1] = dve_done(dve.tensor_tensor(left[:, i - 1, 1:], R[:, i, 0:T], mn[:, (i - 1) % MR, :], ALU.is_lt))
                if i < T:
                    after(dve, m_min[i], row_dd[i])
                    m_scan[i] = dve_done(dve.tensor_tensor_scan(R[:, i + 1, 1:], mn[:, i % MR, :], dd[:, i, :],
                                                                BIG if i else 0.0, ALU.min, ALU.add))
                if i >= LAG:
                    choose(i - LAG)
                if i < T and i % BR == BR - 1:
                    column_of(i // BR)
                    column_end(i // BR)
                    if i // BR < SLOTS:
                        high_parts(NE - i // BR)
                if i >= LAG and (i - LAG) % BR == BR - 1:
                    spread((i - LAG) // BR)
                    steps((i - LAG) // BR)

            l = load(sp, rt_raw[:, :], router, "rt_in")
            after(act, l)
            m = act_done(act.copy(rt_2[:, 0, :], rt_raw[:, :]))
            after(pool, m)
            m_rt = pool_done(pool.tensor_tensor(rt_2[:, 1, :], rt_raw[:, :], rt_2[:, 0, :].bitcast(F32), ALU.subtract))
            for e in range(NE, -1, -1):
                low_parts(e)
                if e - SLOTS >= 0:
                    fetch(e - SLOTS)
                    high_parts(e - SLOTS)

            m = None
            for i in range(T - 1, 0, -1):
                after(dve, m, m_dF[i // BR], m_iota, m_pads)
                m = dve_done(dve.scalar_tensor_tensor(junk[:, :], four[0:Q, :], W[:, i + 1:i + 2], dF[:, i, :], ALU.is_le, ALU.mult,
                                                      accum_out=W[:, i:i + 1]))
            after(dve, m)
            for k in range(2):
                m = dve_done(dve.tensor_copy(Wd[:, k, :, :], W[:, None, k:k + T].to_broadcast([Q, 2, T])))
            WT = bank[0]
            after(pe, m, m_ident)
            for k in range(2):
                m = pe_done(pe.transpose(WT[:, k * Q:(k + 1) * Q], Wd[:, k, :, :].rearrange("q a i -> q (a i)"), ident[0:Q, 0:Q]))
            after(dve, m)
            wt = WT[:, 0:2 * Q].rearrange("p (k n h) -> p k n h", k=2, h=2)
            dve_done(dve.tensor_scalar(bounds[0:T, :, :], wt[0:T, :, :, 0], 0.25, None, ALU.mult))
            m_bounds = dve_done(dve.tensor_scalar(bounds[T:P, :, :], wt[T:P, :, :, 1], 0.25, float(T), ALU.mult, ALU.add))
            stage2_end = [(t.sem, t.n) for t in (pe_done, dve_done, act_done, pool_done)]

        mk = sb("mk", [P, 2, CT, P])
        xT_hi = sb("xT_hi", [P, TOK], F32R)
        xT_lo = sb("xT_lo", [P, TOK], F32R)
        pay = sb("pay", [P, NT, ROW])
        middle = sb("middle", [P, NT])
        reach = sb("reach", [P, NT])
        shift = sb("shift", [P, NT])
        fetch_table(ACT.Sigmoid)
        for e in (pe, dve, act, pool, sp):
            after(e, *stage2_end)
        m_id = pool_done(pool.iota(pay[:, :, D + 1:].bitcast(I32), [[P, NT], [1, 1]], base=0, channel_multiplier=1))
        ALIGN, X_T, LOGIT = bank[1:3], bank[6:8], bank[0]

        m = dve_done(dve.tensor_tensor(middle[:, :], bounds[:, 0, :], bounds[:, 1, :], ALU.add))
        m2 = dve_done(dve.tensor_tensor(reach[:, :], bounds[:, 1, :], bounds[:, 0, :], ALU.subtract))
        after(dve, m)
        m_mid = dve_done(dve.tensor_scalar(middle[:, :], middle[:, :], -0.5, None, ALU.mult))
        after(dve, m2)
        m_reach = dve_done(dve.tensor_scalar(reach[:, :], reach[:, :], 0.5, 0.125, ALU.mult, ALU.add))

        def aligned(c):
            b = c % 2
            s = slice(c * CT, (c + 1) * CT)
            after(act, m_mid, m_iota, old("al", c - 2))
            for t in range(CT):
                m = act_done(act.activation(mk[:, b, t, :], iota_f[:, :], ACT.Abs, bias=middle[:, c * CT + t:c * CT + t + 1]))
            yield
            after(dve, m, m_reach)
            for t in range(CT):
                n = c * CT + t
                m_mk = dve_done(dve.tensor_scalar(mk[:, b, t, :], mk[:, b, t, :], reach[:, n:n + 1], None, ALU.is_le))
            after(pe, m_mk, old("x2", c - 2))
            for t in range(CT):
                m = pe_done(pe.matmul(ALIGN[b][:, t * D:(t + 1) * D], mk[:, b, t, :], cn[:, c * CT + t, :], start=True, stop=True))
            mark("al", c, m)
            yield
            after(dve, m)
            m_x2 = mark("x2", c, dve_done(dve.tensor_tensor(xr[:, s, :], ALIGN[b][:, :].rearrange("p (t d) -> p t d", d=D), xr[:, s, :], ALU.add)))
            m_st = ln_stats(2, c, m_x2)
            after(pool, m_st)
            m = pool_done(pool.tensor_tensor(shift[:, s], mvs[:, 2, s, 0], rstds[:, 2, s], ALU.mult))
            after(pool, m, m_minus)
            m_st = pool_done(pool.tensor_tensor(shift[:, s], shift[:, s], minus[:, s], ALU.mult))
            yield
            after(act, m_st)
            for t in range(CT):
                n = c * CT + t
                m_n = act_done(act.activation(pay[:, n, 0:D], xr[:, n, :], ACT.Identity, bias=shift[:, n:n + 1], scale=rstds[:, 2, n:n + 1]))
            after(pe, m_n, old("xT_lo", c - 2))
            for t in range(CT):
                m = pe_done(pe.transpose(X_T[b][:, t * P:(t + 1) * P], pay[:, c * CT + t, 0:D], ident[:, :]))
            yield
            a = slice(c * CW, (c + 1) * CW)
            after(act, m)
            m_hi = mark("xT_hi", c, act_done(act.copy(xT_hi[:, a], X_T[b][:, :])))
            after(dve, m_hi)
            m_lo = mark("xT_lo", c, dve_done(dve.tensor_tensor(xT_lo[:, a], X_T[b][:, :], xT_hi[:, a].bitcast(F32), ALU.subtract)))
            after(pe, m_lo, m_hi, m_rt)
            for t in range(CT):
                n = c * CT + t
                r = slice(n * P, (n + 1) * P)
                o = LOGIT[:, n * 2 * (NE + 1):(n + 1) * 2 * (NE + 1)]
                pe.matmul(o, xT_hi[:, r], rt_2[:, :, :], start=True, stop=False, skip_group_check=True)
                m = pe_done(pe.matmul(o[:, 0:NE + 1], xT_lo[:, r], rt_2[:, 0, :], start=False, stop=True, skip_group_check=True))
            mark("logit", c, m)

        under_way, started = [], 0
        while under_way or started < NC:
            if started < NC:
                under_way.append(aligned(started))
                started += 1
            under_way = [g for g in under_way[::-1] if next(g, "end") != "end"][::-1]

        xs = sb("xs", [P, 2, D])
        meta = sb("meta", [P, NS, 2])
        slot = sb("slot", [P, 4, 2])
        number = sb("number", [P, 4, 1])
        h_hi = sb("h_hi", [P, 2, KC, CW], F32R)
        h_lo = sb("h_lo", [P, 2, KC, CW], F32R)
        xs_hi = sb("xs_hi", [P, 2, P], F32R)
        xs_lo = sb("xs_lo", [P, 2, P], F32R)

        class Region:

            def __init__(self, a):
                self.flat, self.at = a[:, :, :].rearrange("p n d -> p (n d)"), 0

            def take(self, *shape, parts=P):
                n = int(np.prod(shape))
                a = self.flat[0:parts, self.at:self.at + n]
                self.at += n
                assert self.at <= NT * D
                names = " ".join("abc"[:len(shape)])
                return a.rearrange(f"p ({names}) -> p {names}", **dict(zip(names.split(), shape))) if len(shape) > 1 else a

        context_rows, router_rows = Region(cn), Region(loan)
        g = context_rows.take(2, CW)
        h32 = context_rows.take(KC, CW)
        y = context_rows.take(4, D)
        base_rows = context_rows.take(4, D)

        stage3_end = [(tr.sem, tr.n) for tr in (pe_done, dve_done, act_done)]
        for e in (pe, dve, act):
            after(e, *stage3_end)
        A, U, Y, HT = bank[2:5:2], bank[3:6:2], bank[6:8], bank[0:2]
        free = {}

        def three(o, lhs, rhs):
            (lh, ll), (rh, rl) = lhs, rhs
            return [(o, lh, rh), (o, lh, rl), (o, ll, rh)]

        def products(ps):
            for k, (o, l, r) in enumerate(ps):
                ins = pe.matmul(o, l, r, start=(k == 0), stop=(k == len(ps) - 1))
            return ins

        def down(o, pieces):
            for k, (hh, hl, w) in enumerate(pieces):
                pe.matmul(o, hh, w, start=(k == 0), stop=False, skip_group_check=True)
                ins = pe.matmul(o[:, 0:D], hl, w[:, 0:D], start=False, stop=(k == KC - 1), skip_group_check=True)
            return ins

        def shared(c):
            b = c % 2
            a = slice(c * CW, (c + 1) * CW)
            xT = (xT_hi[:, a], xT_lo[:, a])

            def up(k):
                kw, i = KW[k], (c * KC + k) % 2
                after(pe, m_split[SH], free.get(("U", i)))
                wa = slice(k * P, k * P + kw)
                wu = slice(HID + k * P, HID + k * P + kw)
                m_a = pe_done(products(three(A[i][0:kw, :], (w13_hi[:, SH, wa], w13_lo[:, SH, wa]), xT)))
                m_u = pe_done(products(three(U[i][0:kw, :], (w13_hi[:, SH, wu], w13_lo[:, SH, wu]), xT)))
                after(act, m_a, free.get(("g", i)))
                return m_u, act_done(act.activation(g[0:kw, i, :], A[i][0:kw, :], ACT.Silu))

            def multiply(k, m_u, m_g):
                kw, i = KW[k], (c * KC + k) % 2
                after(dve, m_g, m_u, free.get(("h32", k)))
                m = free[("U", i)] = free[("g", i)] = dve_done(dve.tensor_tensor(h32[0:kw, k, :], U[i][0:kw, :], g[0:kw, i, :], ALU.mult))
                after(act, m, free.get(("h", b)) if k == 0 else None)
                return act_done(act.copy(h_hi[0:kw, b, k, :], h32[0:kw, k, :]))

            def low_part(k, m_hi):
                kw, i = KW[k], (c * KC + k) % 2
                after(dve, m_hi)
                free[("h32", k)] = dve_done(dve.tensor_tensor(h_lo[0:kw, b, k, :], h32[0:kw, k, :], h_hi[0:kw, b, k, :].bitcast(F32), ALU.subtract))
                return free[("h32", k)]

            m_up = [None] * KC
            m_up[0] = up(0)
            yield
            m_up[1] = up(1)
            hi = multiply(0, *m_up[0])
            yield
            m_up[2] = up(2)
            hi, before = multiply(1, *m_up[1]), hi
            low_part(0, before)
            yield
            hi, before = multiply(2, *m_up[2]), hi
            low_part(1, before)
            yield
            m_lo = low_part(2, hi)
            yield
            after(pe, m_lo, free.get("Y"))
            for t in range(CT):
                r = slice(t * P, (t + 1) * P)
                yb = Y[t // 2][:, (t % 2) * 2 * D:(t % 2 + 1) * 2 * D]
                m = pe_done(down(yb, [(h_hi[0:KW[k], b, k, r], h_lo[0:KW[k], b, k, r], w2_2[0:KW[k], SH, k, :, :].rearrange("p a d -> p (a d)"))
                                      for k in range(KC)]))
            free[("h", b)] = m
            yield
            assert "m_ws" in done
            after(dve, m, done["m_ws"])
            ms = []
            for part in range(2):
                for t in range(CT):
                    n = c * CT + t
                    if part:
                        after(dve, ms[t])
                    yb = Y[t // 2][:, (2 * (t % 2) + part) * D:(2 * (t % 2) + part + 1) * D]
                    m = dve_done(dve.scalar_tensor_tensor(xr[:, n, :], yb, w_sh[:, n:n + 1], xr[:, n, :], ALU.mult, ALU.add))
                    ms.append(m)
            free["Y"] = m
            mark("x3", c, m)

        x3_out = []

        def store_x3():
            while old("x3", len(x3_out)):
                c = len(x3_out)
                after(sp, old("x3", c))
                s = slice(c * CT, (c + 1) * CT)
                x3_out.append(load(sp, x3.rearrange("(n p) d -> p n d", p=P)[:, s, :], xr[:, s, :], f"x3_out{c}"))

        done = {}
        shared_run = {"next": 0, "rounds": 0, "under_way": []}

        def shared_round():
            r = shared_run
            if r["rounds"] % KC == 0 and r["next"] < NC:
                r["under_way"].append(shared(r["next"]))
                r["next"] += 1
            r["under_way"] = [gen for gen in r["under_way"][::-1] if next(gen, "end") != "end"][::-1]
            r["rounds"] += 1
            return r["under_way"] or r["next"] < NC

        lg, pr, oh, key, t1 = (router_rows.take(NT, NE) for _ in range(5))
        cnt, incl, base, lt = (router_rows.take(NE, NT) for _ in range(4))
        pm, km, sc, inv, pos = (router_rows.take(NT) for _ in range(5))
        te, ends = (router_rows.take(NE) for _ in range(2))
        ekc = router_rows.take(NS, NE - 1, parts=1)
        ekf = router_rows.take(NS, parts=1)
        oh_b = sb("oh_b", [P, NT, NE], BF16)
        RANK, COUNT = bank[1], bank[1][:, 256:512]
        steps_done = [0]

        after(dve, old("logit", NC - 1), m_rb, m_split[0])
        lgp = LOGIT[:, :].rearrange("p (n a e) -> p n a e", a=2, e=NE + 1)[:, :, :, 0:NE]

        def chain(ins):
            m = dve_done(ins)
            steps_done[0] += 1
            if steps_done[0] in ROUNDS_AT:
                shared_round()
            after(dve, m)
            return m

        ROUNDS_AT = (6, 9, 12, 15, 18, 21, 24)

        def over_e(a):
            return a[:, :, None].to_broadcast([P, NT, NE])

        chain(dve.tensor_tensor(lg[:, :, :], lgp[:, :, 0, :], rb[:, None, :].to_broadcast([P, NT, NE]), ALU.add))
        chain(dve.tensor_tensor(lg[:, :, :], lgp[:, :, 1, :], lg[:, :, :], ALU.add))
        m = chain(dve.tensor_scalar(lg[:, :, :], lg[:, :, :], -50.0, 50.0, ALU.max, ALU.min))
        after(act, m)
        m = act_done(act.activation(pr[:, :, :], lg[:, :, :], ACT.Sigmoid))
        shared_round()
        after(dve, m)
        chain(dve.tensor_reduce(pm[:, :], pr[:, :, :], AX_X, ALU.max))
        chain(dve.tensor_tensor(oh[:, :, :], pr[:, :, :], over_e(pm), ALU.is_equal))
        chain(dve.tensor_tensor(key[:, :, :], oh[:, :, :], prio[:, None, :].to_broadcast([P, NT, NE]), ALU.mult))
        chain(dve.tensor_reduce(km[:, :], key[:, :, :], AX_X, ALU.max))
        m_oh = chain(dve.tensor_tensor(oh_b[:, :, :], key[:, :, :], over_e(km), ALU.is_equal))
        ohf = oh_b[:, :, :].rearrange("p n e -> p (n e)")
        after(pe, m_oh, m_tri)
        pe_done(pe.matmul(RANK[:, 0:NT * NE], tri[:, :], ohf, start=True, stop=True))
        m_rank = pe_done(pe.matmul(COUNT[:, 0:NT * NE], ones[:, :], ohf, start=True, stop=True))
        chain(dve.tensor_scalar(pm[:, :], pm[:, :], 1e-8, 1.0 - 1e-8, ALU.max, ALU.min))
        chain(dve.tensor_scalar(sc[:, :], pm[:, :], 0.5, 1e-8, ALU.add, ALU.add))
        chain(dve.tensor_scalar(sc[:, :], sc[:, :], 0.5, 2.0, ALU.max, ALU.min))
        chain(dve.reciprocal(inv[:, :], sc[:, :]))
        chain(dve.tensor_tensor(pay[:, :, D], pm[:, :], inv[:, :], ALU.mult))
        m_ws = done["m_ws"] = chain(dve.tensor_scalar(w_sh[:, :], inv[:, :], 0.5, None, ALU.mult))
        after(dve, m_rank)
        chain(dve.tensor_copy(cnt[:, :, :], COUNT[:, 0:NT * NE].rearrange("p (n e) -> p e n", e=NE)))
        chain(dve.tensor_tensor_scan(incl[:, :, :].rearrange("p e n -> p (e n)"), carry[:, :, :].rearrange("p e n -> p (e n)"),
                                     cnt[:, :, :].rearrange("p e n -> p (e n)"), 0.0, ALU.mult, ALU.add))
        chain(dve.tensor_tensor(lt[:, :, :], i128[:, None, 0:NT].to_broadcast([P, NE, NT]),
                                incl[:, :, NT - 1:NT].to_broadcast([P, NE, NT]), ALU.is_lt))
        chain(dve.tensor_reduce(te[:, :], lt[:, :, :], AX_X, ALU.add))
        m_ends = chain(dve.tensor_tensor_scan(ends[:, :], onesf[:, 0:NE], te[:, :], 0.0, ALU.mult, ALU.add))
        chain(dve.tensor_tensor(te[:, :], ends[:, :], te[:, :], ALU.subtract))
        chain(dve.tensor_tensor(base[:, :, :], incl[:, :, :], cnt[:, :, :], ALU.subtract))
        chain(dve.scalar_tensor_tensor(base[:, :, :], te[:, :, None].to_broadcast([P, NE, NT]), float(P), base[:, :, :], ALU.mult, ALU.add))
        chain(dve.tensor_tensor(t1[:, :, :], RANK[:, 0:NT * NE].rearrange("p (n e) -> p n e", e=NE),
                                base[:, :, :].rearrange("p e n -> p n e"), ALU.add))
        chain(dve.tensor_tensor(t1[:, :, :], t1[:, :, :], oh_b[:, :, :], ALU.mult))
        chain(dve.tensor_reduce(pos[:, :], t1[:, :, :], AX_X, ALU.add))
        m_pos = chain(dve.tensor_copy(pos_i[:, :], pos[:, :]))
        chain(dve.tensor_tensor(ekc[:, :, :], ends[0:1, None, 0:NE - 1].to_broadcast([1, NS, NE - 1]),
                                iota_f[0:1, 0:NS, None].to_broadcast([1, NS, NE - 1]), ALU.is_le))
        chain(dve.tensor_reduce(ekf[:, :], ekc[:, :, :], AX_X, ALU.add))
        chain(dve.tensor_scalar(up_at[:, 0:NS], ekf[:, :], float(2 * HID), None, ALU.mult))
        m_ek = chain(dve.tensor_scalar(down_at[:, 2:NS + 2], ekf[:, :], float(KC * 2 * D), None, ALU.mult))

        s_put = sem("s_put")
        after(pool, m_pos, m_fill, m_id)
        for n in range(NT):
            pool.indirect_dma_start(routed, bass.IndirectOffsetOnAxis(ap=pos_i[:, n:n + 1], axis=0), pay[:, n, :], None,
                                    bounds_check=NS * P - 1).then_inc(s_put, 16)
        m_put = (s_put, NT * 16)

        store_x3()
        after(sp, m_put)
        m_meta = load(sp, meta[:, :, :], routed.rearrange("(k p) r -> p k r", p=P)[:, :, D:], "meta_in")

        s_x, s_xh, s_xl, s_a, s_u, s_g, s_h, s_t, s_hh, s_hl, s_y, s_ys, s_rn, s_y1 = (sem("tile_" + n) for n in
            ("x", "x_hi", "x_lo", "a", "u", "silu", "h", "hT", "hT_hi", "hT_lo", "y", "y_out", "row_no", "y_part"))
        s_xi = [sem("tile_in0"), sem("tile_in1")]
        s_o = [sem(f"tile_put{k}") for k in range(4)]
        s_b = [sem(f"tile_base{k}") for k in range(4)]
        X = [hb[:, CW - P:] for hb in HT]
        out_rows = out.rearrange("b t d -> (b t) d")

        def cols(start, n):
            return slice(start, start + n) if isinstance(start, int) else bass.ds(start, n)

        meta_flat = meta[:, :, :].rearrange("p k r -> p (k r)")

        def x_load(k, i, again):
            if again:
                sp.wait_ge(s_x, k - 1)
            sp.dma_start(xs[:, i, :], routed[cols(k * P, P), 0:D]).then_inc(s_xi[i], 16)

        def x_turn(k, i, pair):
            pe.wait_ge(s_xi[i], (pair + 1) * 16)
            pe.transpose(X[1 - i], xs[:, i, :], ident[:, :]).then_inc(s_x, 1)

        w13_flat_hi = w13_hi[:, :, :].rearrange("p e h -> p (e h)")
        w13_flat_lo = w13_lo[:, :, :].rearrange("p e h -> p (e h)")
        w2_flat = w2_2[:, :, :, :, :].rearrange("p e k a d -> p (e k a d)")

        def x_high(k, i):
            act.wait_ge(s_x, k + 1)
            act.copy(xs_hi[:, i, :], X[1 - i]).then_inc(s_xh, 1)

        def x_low(k, i):
            dve.wait_ge(s_xh, k + 1)
            dve.tensor_tensor(xs_lo[:, i, :], X[1 - i], xs_hi[:, i, :].bitcast(F32), ALU.subtract).then_inc(s_xl, 1)

        def routed_step(s, j4, pair, do, blk=None):
            i = j4 % 2
            j = 1 - i
            if "up" in do:
                base = expert_at(up_reg[j4], 2 * HID)
                pe.wait_ge(s_xl, s + 1)
                if "up again" in do:
                    pe.wait_ge(s_h, s - 1)
                xT = (xs_hi[:, i, :], xs_lo[:, i, :])
                for o, off, sg in ((A[i], 0, s_a), (U[i], HID, s_u)):
                    hi = w13_flat_hi[:, bass.ds(base + off, HID)]
                    lo = w13_flat_lo[:, bass.ds(base + off, HID)]
                    products(three(o[:, 0:HID], xT, (hi, lo))).then_inc(sg, 1)
            if j4 == 0:
                pe.load(down_reg, down_at[0:1, cols(s, 4)])
            if j4 == 3:
                pe.load(up_reg, up_at[0:1, cols(s + 1, 4)])
            if "turn" in do:
                if "turn again" in do:
                    pe.wait_ge(s_hl, s - 2)
            if "x" in do:
                x_turn(s + 2, i, pair + 1)
            if "turn" in do:
                pe.wait_ge(s_h, s)
                for k in range(KC):
                    ins = pe.transpose(HT[j][0:KW[k], k * P:(k + 1) * P], g[:, j, k * P:k * P + KW[k]], ident[:, :])
                ins.then_inc(s_t, 1)
            if "down" in do:
                base = expert_at(down_reg[j4], KC * 2 * D)
                pe.wait_ge(s_hl, s - 1)
                if "down again" in do:
                    pe.wait_ge(s_ys, s - 3)
                down(Y[i][:, 0:2 * D], [(h_hi[0:KW[k], i, k, 0:P], h_lo[0:KW[k], i, k, 0:P], w2_flat[0:KW[k], bass.ds(base + k * 2 * D, 2 * D)])
                                        for k in range(KC)]).then_inc(s_y, 1)
            if "up" in do:
                act.wait_ge(s_a, s + 1)
                if "up again" in do:
                    act.wait_ge(s_t, s - 1)
                act.activation(g[:, i, 0:HID], A[i][:, 0:HID], ACT.Silu).then_inc(s_g, 1)
                dve.wait_ge(s_u, s + 1)
                dve.wait_ge(s_g, s + 1)
                dve.tensor_tensor(g[:, i, 0:HID], U[i][:, 0:HID], g[:, i, 0:HID], ALU.mult).then_inc(s_h, 1)
            if "turn" in do:
                act.wait_ge(s_t, s)
            if "x" in do:
                x_high(s + 2, i)
                if "turn" not in do:
                    x_low(s + 2, i)
            if "turn" in do:
                if "turn again" in do:
                    act.wait_ge(s_y, s - 2)
                act.copy(h_hi[:, j, 0:2, 0:P], HT[j][:, 0:2 * P].rearrange("p (k t) -> p k t", k=2)).then_inc(s_hh, 1)
                act.copy(h_hi[0:KW[2], j, 2, 0:P], HT[j][0:KW[2], 2 * P:3 * P]).then_inc(s_hh, 1)
                dve.wait_ge(s_hh, s * 2)
                if "x" in do:
                    x_low(s + 2, i)
                dve.tensor_tensor(h_lo[:, j, 0:2, 0:P], HT[j][:, 0:2 * P].rearrange("p (k t) -> p k t", k=2),
                                  h_hi[:, j, 0:2, 0:P].bitcast(F32), ALU.subtract)
                dve.tensor_tensor(h_lo[0:KW[2], j, 2, 0:P], HT[j][0:KW[2], 2 * P:3 * P],
                                  h_hi[0:KW[2], j, 2, 0:P].bitcast(F32), ALU.subtract).then_inc(s_hl, 1)
            if "down" in do:
                dve.wait_ge(s_rn, s - 1)
                dve.wait_ge(s_y, s - 1)
                k4 = (j4 - 2) % 4
                weight = slot[:, k4, 0:1]
                turns = (s - 2) // 4 + 1 if isinstance(s, int) else blk if j4 < 2 else blk + 1
                dve.wait_ge(s_b[k4], turns * 16)
                if "put again" in do:
                    dve.wait_ge(s_o[k4], turns * 16 - 16)
                dve.scalar_tensor_tensor(y[:, k4, :], Y[i][:, 0:D], weight, base_rows[:, k4, :], ALU.mult, ALU.add).then_inc(s_y1, 1)
                dve.tensor_copy(number[:, k4, :], meta_flat[:, cols((s - 2) * 2 + 1, 1)])
            if "up" in do:
                dve.tensor_copy(slot[:, j4, :], meta_flat[:, cols(s * 2, 2)]).then_inc(s_rn, 1)
                if isinstance(s, int):
                    pool.wait_ge(s_rn, s + 1)
                else:
                    pool.wait_ge(s_rn, slot_due)
                    pool.reg_add(slot_due, slot_due, 1)
                pool.indirect_dma_start(base_rows[:, j4, :], None, x3, bass.IndirectOffsetOnAxis(ap=slot[:, j4, 1:2].bitcast(U32), axis=0),
                                        bounds_check=TOK - 1, oob_is_err=False).then_inc(s_b[j4], 16)
            if "down" in do:
                dve.wait_ge(s_y1, s - 1)
                dve.scalar_tensor_tensor(y[:, k4, :], Y[i][:, D:2 * D], weight, y[:, k4, :], ALU.mult, ALU.add).then_inc(s_ys, 1)
                if isinstance(s, int):
                    pool.wait_ge(s_ys, s - 1)
                else:
                    pool.wait_ge(s_ys, y_due)
                    pool.reg_add(y_due, y_due, 1)
                pool.indirect_dma_start(out_rows, bass.IndirectOffsetOnAxis(ap=number[:, k4, :].bitcast(U32), axis=0),
                                        y[:, k4, :], None, bounds_check=TOK - 1, oob_is_err=False).then_inc(s_o[k4], 16)
            if "load" in do:
                x_load(s + 4, i, True)

        m_base = pool_done(pool.memset(base_rows[:, :, :], 0.0))
        for k in range(2):
            x_load(k, k, False)
        store_x3()
        while shared_run["rounds"] < (NC - 1) * KC + 5:
            shared_round()
        after(pe, m_ek, m_pos)
        for k in range(2):
            x_turn(k, k, 0)
            x_high(k, k)
            x_low(k, k)
            x_load(k + 2, k, True)
        while shared_round():
            pass
        store_x3()
        after(dve, m_meta)
        after(pool, m_meta, *x3_out, m_base)

        slot_due = pool.alloc_register("slot_due")
        y_due = pool.alloc_register("y_due")
        up_reg = [pe.alloc_register(f"up_expert{k}") for k in range(4)]
        down_reg = [pe.alloc_register(f"down_expert{k}") for k in range(4)]

        def expert_at(reg, step):
            return pe.snap(reg, min_val=0, max_val=(NE - 1) * step)

        def parts(s):
            has = {"up": s < NS, "up again": 2 <= s, "turn": 1 <= s <= NS, "turn again": 3 <= s, "down": 2 <= s,
                   "down again": 4 <= s, "put again": 6 <= s, "x": s + 2 < NS, "load": s + 4 < NS}
            return {k for k, yes in has.items() if yes}

        pe.load(up_reg, up_at[0:1, 0:4])
        last_use = {0: [free[(n, i)] for n in ("U", "g") for i in range(2)],
                    1: [free[("h", i)] for i in range(2)],
                    2: [free["Y"]]}
        FIRST = 2
        for s in range(FIRST * 4):
            after(pe, *last_use.get(s, []))
            after(act, *last_use.get(s, []))
            routed_step(s, s % 4, s // 2, parts(s))
        END = (NS - 4) // 4
        pool.reg_mov(y_due, FIRST * 4 - 1)
        pool.reg_mov(slot_due, FIRST * 4 + 1)
        with nc.Fori(FIRST, END) as blk:
            for j4 in range(4):
                routed_step(blk * 4 + j4, j4, blk * 2 + j4 // 2, parts(FIRST * 4), blk)
        for s in range(END * 4, NS + 2):
            routed_step(s, s % 4, s // 2, parts(s))

        after(sp, *((s_o[k], 16 * len(range(k, NS, 4))) for k in range(4)))


_OUTS = [((64, 64, 128), "float32")]


def kernel(**inputs):
    import numpy as _np
    import concourse.bacc as _bacc
    from concourse import mybir as _mybir
    from concourse.bass_utils import run_bass_kernel_spmd as _run

    g = {k.replace("L0_", ""): _np.asarray(v) for k, v in inputs.items()}
    w1 = _np.concatenate([g["ffn_ew1"], g["ffn_sw1"][None]])
    w3 = _np.concatenate([g["ffn_ew3"], g["ffn_sw3"][None]])
    w2 = _np.concatenate([g["ffn_ew2"], g["ffn_sw2"][None]])
    w13 = _np.concatenate([w1, w3], axis=1).transpose(2, 0, 1)
    w2p = _np.zeros((NE + 1, D, KC * P), w2.dtype)
    w2p[:, :, :HID] = w2
    w2p = w2p.reshape(NE + 1, D, KC, P).transpose(3, 0, 2, 1)
    rt = _np.zeros((D, NE + 1), g["ffn_router_w"].dtype)
    rt[:, :NE] = g["ffn_router_w"].T
    args_np = {
        "x": g["x"], "ctx": g["ctx_1024"], "ctxT": g["ctx_1024"].reshape(TOK, D).T,
        "w_inT": g["attn_W_in"].T, "b_in": g["attn_b_in"].reshape(2, D).T, "w_sT": g["attn_W_s"].T, "b_s": g["attn_b_s"].reshape(1, D).T,
        "w_oT": g["attn_W_o"].T, "b_o": g["attn_b_o"], "router": rt, "r_bias": g["ffn_routing_bias"],
        "w13": w13, "w2": w2p,
    }
    nc = _bacc.Bacc("TRN2", target_bir_lowering=False, num_devices=1)
    arrays, args = {}, []
    for name, a in args_np.items():
        a = _np.ascontiguousarray(a)
        arrays[f"in_{name}"] = a
        args.append(nc.dram_tensor(f"in_{name}", a.shape, _mybir.dt.from_np(a.dtype), kind="ExternalInput").ap())
    args.append(nc.dram_tensor("out_0", (64, 64, 128), _mybir.dt.float32, kind="ExternalOutput").ap())
    program(nc, *args)
    r = _run(nc, [arrays], core_ids=[0])
    return r.results[0]["out_0"]
```
